# Optimizing a Trainium2 kernel written in Bass

```python
import numpy as np
import jax
import jax.numpy as jnp

def _softmax(x, axis=-1):
    return jax.nn.softmax(x, axis=axis)

def _gelu(x):
    return jax.nn.gelu(x, approximate=True)

def _silu(x):
    return jax.nn.silu(x)

def _sigmoid(x):
    return jax.nn.sigmoid(x)

def _layernorm(x, axis=-1, eps=1e-05):
    m = jnp.mean(x, axis=axis, keepdims=True)
    v = jnp.var(x, axis=axis, keepdims=True)
    return (x - m) / jnp.sqrt(v + eps)

def _scatter_add(tgt, idx, src, axis=0):
    return tgt.at[idx].add(src)

def _segment_sum(src, seg, n):
    return jax.ops.segment_sum(src, seg, n)
kernel_name = 'mk_vit_tower_postln_d2_tok_img768_r4_09508d'

def setup_inputs(seed: int=0):
    np.random.seed(seed)
    _w = jnp.asarray

    def _rec_inputs():
        import jax
        import jax.numpy as jnp
        _rk = jax.random.key(seed)
        x = -0.000137204 + 0.999937 * jax.random.normal(jax.random.fold_in(_rk, 1), (64, 3, 112, 112), jnp.float32)
        return x
    x = _rec_inputs()

    def _L0_tok_setup():
        import jax, jax.numpy as jnp
        import numpy as np
        B, C, H, W_IMG = (128, 3, 224, 224)
        N_PATCH, EMBED = (256, 192)
        GRID = 32
        key = jax.random.key(seed)
        k1, k2, k3, k4 = jax.random.split(key, 4)
        x = jax.random.normal(k1, (B, C, H, W_IMG), dtype=jnp.float32)
        curve = jax.random.randint(k2, (N_PATCH, 2), 0, GRID, dtype=jnp.int32)
        proj_w = jax.random.normal(k3, (EMBED, C), dtype=jnp.float32) * 0.02
        proj_b = jax.random.normal(k4, (EMBED,), dtype=jnp.float32) * 0.02
        return {'x': x, 'curve': curve, 'proj_w': proj_w, 'proj_b': proj_b}
    _L0_tok_all = _L0_tok_setup()
    _L0_tok_in = {k: v for k, v in _L0_tok_all.items() if k in ('curve', 'proj_w', 'proj_b')}
    del _L0_tok_all

    def _L0_attn_setup():
        import jax, jax.numpy as jnp
        import numpy as np
        B_, L_, DM = (2, 512, 192)
        DS, DC, EXP = (32, 7, 2)
        DI = EXP * DM
        EPS = 1e-05

        def _mamba_forward(x, Win, conv_w, conv_b, Wx, A_log, D, Wout, ln_g, ln_b):
            residual = x
            mu = jnp.mean(x, axis=-1, keepdims=True)
            var = jnp.var(x, axis=-1, keepdims=True)
            xn = (x - mu) / jnp.sqrt(var + EPS) * ln_g + ln_b
            xz = xn @ Win.T
            xc, z = jnp.split(xz, 2, axis=-1)
            xt = jnp.moveaxis(xc, 1, 2)
            conv = jax.lax.conv_general_dilated(xt, conv_w, window_strides=(1,), padding=[(DC - 1, 0)], dimension_numbers=('NCH', 'OIH', 'NCH'), feature_group_count=DI)
            conv = conv + conv_b[None, :, None]
            xc = jax.nn.silu(jnp.moveaxis(conv, 1, 2))
            xp = xc @ Wx.T
            Bm = xp[..., :DS]
            Cm = xp[..., DS:2 * DS]
            delta = jax.nn.softplus(xp[..., 2 * DS:])
            A = -jnp.exp(A_log)
            dA = jnp.exp(delta[..., None] * A)
            dBx = (delta * xc)[..., None] * Bm[:, :, None, :]

            def step(h, inp):
                dA_t, dBx_t, C_t = inp
                h = dA_t * h + dBx_t
                y = jnp.einsum('bdn,bn->bd', h, C_t)
                return (h, y)
            h0 = jnp.zeros((x.shape[0], DI, DS), xc.dtype)
            xs = (jnp.moveaxis(dA, 1, 0), jnp.moveaxis(dBx, 1, 0), jnp.moveaxis(Cm, 1, 0))
            _, ys = jax.lax.scan(step, h0, xs)
            y = jnp.moveaxis(ys, 0, 1) + xc * D
            y = y * jax.nn.silu(z)
            return y @ Wout.T + residual
        key = jax.random.key(seed)
        ks = jax.random.split(key, 6)
        sc = lambda k, shp: jax.random.normal(k, shp, jnp.float32) * 0.02
        x = jax.random.normal(ks[0], (B_, L_, DM), jnp.float32)
        Win = sc(ks[1], (2 * DI, DM))
        conv_w = sc(ks[2], (DI, 1, DC))
        conv_b = jnp.zeros((DI,), jnp.float32)
        Wx = sc(ks[3], (2 * DS + DI, DI))
        A_log = jnp.broadcast_to(jnp.log(jnp.arange(1, DS + 1, dtype=jnp.float32)), (DI, DS))
        D = jnp.ones((DI,), jnp.float32)
        Wout = sc(ks[4], (DM, DI))
        ln_g = jnp.ones((DM,), jnp.float32)
        ln_b = jnp.zeros((DM,), jnp.float32)
        return {'x': x, 'Win': Win, 'conv_w': conv_w, 'conv_b': conv_b, 'Wx': Wx, 'A_log': A_log, 'D': D, 'Wout': Wout, 'ln_g': ln_g, 'ln_b': ln_b}
    _L0_attn_all = _L0_attn_setup()
    _L0_attn_in = {k: v for k, v in _L0_attn_all.items() if k in ('Win', 'conv_w', 'conv_b', 'Wx', 'A_log', 'D', 'Wout', 'ln_g', 'ln_b')}
    del _L0_attn_all

    def _L0_ffn_setup():
        import jax, jax.numpy as jnp
        import numpy as np
        key = jax.random.key(seed)
        k1, k2 = jax.random.split(key)
        B, S, D_IN, D_OUT = (4, 2048, 192, 192)
        x = jax.random.normal(k1, (B, S, D_IN), dtype=jnp.float32)
        weight = jax.random.normal(k2, (D_OUT, D_IN), dtype=jnp.float32) * (1.0 / jnp.sqrt(D_OUT))
        return {'x': x, 'weight': weight}
    _L0_ffn_all = _L0_ffn_setup()
    _L0_ffn_in = {k: v for k, v in _L0_ffn_all.items() if k in ('weight',)}
    del _L0_ffn_all

    def _L1_attn_setup():
        import jax, jax.numpy as jnp
        import numpy as np
        B, L, D_MODEL = (2, 1024, 192)
        D_STATE, D_CONV, EXPAND = (16, 4, 2)
        E = EXPAND * D_MODEL
        LN_EPS = 1e-05
        key = jax.random.key(seed)
        ks = jax.random.split(key, 8)
        s = lambda k, shape, scale: jax.random.normal(k, shape, jnp.float32) * scale
        return {'x': jax.random.normal(ks[0], (B, L, D_MODEL), jnp.float32), 'ln_g': jnp.ones((D_MODEL,), jnp.float32), 'ln_b': jnp.zeros((D_MODEL,), jnp.float32), 'W_in': s(ks[1], (D_MODEL, E), 0.02), 'b_in': jnp.zeros((E,), jnp.float32), 'W_conv': s(ks[2], (E, 1, D_CONV), 0.1), 'b_conv': jnp.zeros((E,), jnp.float32), 'W_xp': s(ks[3], (E, D_STATE + D_MODEL), 0.02), 'b_xp': jnp.zeros((D_STATE + D_MODEL,), jnp.float32), 'W_dt': s(ks[4], (E, D_STATE), 0.02), 'b_dt': jnp.zeros((D_STATE,), jnp.float32), 'W_us': s(ks[5], (D_STATE, D_MODEL), 0.02), 'b_us': jnp.zeros((D_MODEL,), jnp.float32), 'W_out': s(ks[6], (E, D_MODEL), 0.02), 'b_out': jnp.zeros((D_MODEL,), jnp.float32)}
    _L1_attn_all = _L1_attn_setup()
    _L1_attn_in = {k: v for k, v in _L1_attn_all.items() if k in ('ln_g', 'ln_b', 'W_in', 'b_in', 'W_conv', 'b_conv', 'W_xp', 'b_xp', 'W_dt', 'b_dt', 'W_us', 'b_us', 'W_out', 'b_out')}
    del _L1_attn_all

    def _L1_ffn_setup():
        import jax, jax.numpy as jnp
        import numpy as np
        from jax import lax
        DIM = 192
        INTER = 128
        E = 8
        G = 4
        TOPK_G = 2
        TOPK = 2
        ROUTE_SCALE = 1.0

        def _gate(x2, gate_weight, gate_bias):
            T = x2.shape[0]
            scores = jax.nn.sigmoid(x2 @ gate_weight.T)
            s = scores + gate_bias
            sv = s.reshape(T, G, E // G)
            top2, _ = lax.top_k(sv, 2)
            group_scores = top2.sum(-1)
            _, gidx = lax.top_k(group_scores, TOPK_G)
            gmask = jnp.zeros((T, G), bool).at[jnp.arange(T)[:, None], gidx].set(True)
            masked = jnp.where(gmask[:, :, None], sv, -jnp.inf).reshape(T, E)
            _, idx = lax.top_k(masked, TOPK)
            w = jnp.take_along_axis(scores, idx, axis=1)
            w = w / (w.sum(-1, keepdims=True) + 1e-06) * ROUTE_SCALE
            return (w, idx)
        key = jax.random.key(seed)
        ks = jax.random.split(key, 9)
        s = 1.0 / np.sqrt(DIM)
        si = 1.0 / np.sqrt(INTER)
        return {'x': jax.random.normal(ks[0], (4, 1024, DIM), jnp.float32), 'gate_weight': jax.random.uniform(ks[1], (E, DIM), jnp.float32, -s, s), 'gate_bias': jnp.zeros((E,), jnp.float32), 'w1': jax.random.uniform(ks[2], (E, INTER, DIM), jnp.float32, -s, s), 'w2': jax.random.uniform(ks[3], (E, DIM, INTER), jnp.float32, -si, si), 'w3': jax.random.uniform(ks[4], (E, INTER, DIM), jnp.float32, -s, s), 'sw1': jax.random.uniform(ks[5], (INTER, DIM), jnp.float32, -s, s), 'sw2': jax.random.uniform(ks[6], (DIM, INTER), jnp.float32, -si, si), 'sw3': jax.random.uniform(ks[7], (INTER, DIM), jnp.float32, -s, s)}
    _L1_ffn_all = _L1_ffn_setup()
    _L1_ffn_in = {k: v for k, v in _L1_ffn_all.items() if k in ('gate_weight', 'gate_bias', 'w1', 'w2', 'w3', 'sw1', 'sw2', 'sw3')}
    del _L1_ffn_all
    return {'x': x, 'L0_tok_curve': _L0_tok_in['curve'], 'L0_tok_proj_w': _L0_tok_in['proj_w'], 'L0_tok_proj_b': _L0_tok_in['proj_b'], 'L0_attn_Win': _L0_attn_in['Win'], 'L0_attn_conv_w': _L0_attn_in['conv_w'], 'L0_attn_conv_b': _L0_attn_in['conv_b'], 'L0_attn_Wx': _L0_attn_in['Wx'], 'L0_attn_A_log': _L0_attn_in['A_log'], 'L0_attn_D': _L0_attn_in['D'], 'L0_attn_Wout': _L0_attn_in['Wout'], 'L0_attn_ln_g': _L0_attn_in['ln_g'], 'L0_attn_ln_b': _L0_attn_in['ln_b'], 'L0_ffn_weight': _L0_ffn_in['weight'], 'L1_attn_ln_g': _L1_attn_in['ln_g'], 'L1_attn_ln_b': _L1_attn_in['ln_b'], 'L1_attn_W_in': _L1_attn_in['W_in'], 'L1_attn_b_in': _L1_attn_in['b_in'], 'L1_attn_W_conv': _L1_attn_in['W_conv'], 'L1_attn_b_conv': _L1_attn_in['b_conv'], 'L1_attn_W_xp': _L1_attn_in['W_xp'], 'L1_attn_b_xp': _L1_attn_in['b_xp'], 'L1_attn_W_dt': _L1_attn_in['W_dt'], 'L1_attn_b_dt': _L1_attn_in['b_dt'], 'L1_attn_W_us': _L1_attn_in['W_us'], 'L1_attn_b_us': _L1_attn_in['b_us'], 'L1_attn_W_out': _L1_attn_in['W_out'], 'L1_attn_b_out': _L1_attn_in['b_out'], 'L1_ffn_gate_weight': _L1_ffn_in['gate_weight'], 'L1_ffn_gate_bias': _L1_ffn_in['gate_bias'], 'L1_ffn_w1': _L1_ffn_in['w1'], 'L1_ffn_w2': _L1_ffn_in['w2'], 'L1_ffn_w3': _L1_ffn_in['w3'], 'L1_ffn_sw1': _L1_ffn_in['sw1'], 'L1_ffn_sw2': _L1_ffn_in['sw2'], 'L1_ffn_sw3': _L1_ffn_in['sw3']}

def reference(x, L0_tok_curve, L0_tok_proj_w, L0_tok_proj_b, L0_attn_Win, L0_attn_conv_w, L0_attn_conv_b, L0_attn_Wx, L0_attn_A_log, L0_attn_D, L0_attn_Wout, L0_attn_ln_g, L0_attn_ln_b, L0_ffn_weight, L1_attn_ln_g, L1_attn_ln_b, L1_attn_W_in, L1_attn_b_in, L1_attn_W_conv, L1_attn_b_conv, L1_attn_W_xp, L1_attn_b_xp, L1_attn_W_dt, L1_attn_b_dt, L1_attn_W_us, L1_attn_b_us, L1_attn_W_out, L1_attn_b_out, L1_ffn_gate_weight, L1_ffn_gate_bias, L1_ffn_w1, L1_ffn_w2, L1_ffn_w3, L1_ffn_sw1, L1_ffn_sw2, L1_ffn_sw3):
    import jax
    import jax.numpy as jnp

    def _L0_tok_ref(x, curve, proj_w, proj_b):
        import jax, jax.numpy as jnp
        import numpy as np
        B, C, H, W_IMG = (128, 3, 224, 224)
        N_PATCH, EMBED = (256, 192)
        GRID = 32
        gathered = x[:, :, curve[:, 1], curve[:, 0]]
        return jnp.einsum('bcn,ec->bne', gathered, proj_w) + proj_b

    def _L0_attn_ref(x, Win, conv_w, conv_b, Wx, A_log, D, Wout, ln_g, ln_b):
        import jax, jax.numpy as jnp
        import numpy as np
        B_, L_, DM = (2, 512, 192)
        DS, DC, EXP = (32, 7, 2)
        DI = EXP * DM
        EPS = 1e-05

        def _mamba_forward(x, Win, conv_w, conv_b, Wx, A_log, D, Wout, ln_g, ln_b):
            residual = x
            mu = jnp.mean(x, axis=-1, keepdims=True)
            var = jnp.var(x, axis=-1, keepdims=True)
            xn = (x - mu) / jnp.sqrt(var + EPS) * ln_g + ln_b
            xz = xn @ Win.T
            xc, z = jnp.split(xz, 2, axis=-1)
            xt = jnp.moveaxis(xc, 1, 2)
            conv = jax.lax.conv_general_dilated(xt, conv_w, window_strides=(1,), padding=[(DC - 1, 0)], dimension_numbers=('NCH', 'OIH', 'NCH'), feature_group_count=DI)
            conv = conv + conv_b[None, :, None]
            xc = jax.nn.silu(jnp.moveaxis(conv, 1, 2))
            xp = xc @ Wx.T
            Bm = xp[..., :DS]
            Cm = xp[..., DS:2 * DS]
            delta = jax.nn.softplus(xp[..., 2 * DS:])
            A = -jnp.exp(A_log)
            dA = jnp.exp(delta[..., None] * A)
            dBx = (delta * xc)[..., None] * Bm[:, :, None, :]

            def step(h, inp):
                dA_t, dBx_t, C_t = inp
                h = dA_t * h + dBx_t
                y = jnp.einsum('bdn,bn->bd', h, C_t)
                return (h, y)
            h0 = jnp.zeros((x.shape[0], DI, DS), xc.dtype)
            xs = (jnp.moveaxis(dA, 1, 0), jnp.moveaxis(dBx, 1, 0), jnp.moveaxis(Cm, 1, 0))
            _, ys = jax.lax.scan(step, h0, xs)
            y = jnp.moveaxis(ys, 0, 1) + xc * D
            y = y * jax.nn.silu(z)
            return y @ Wout.T + residual
        return _mamba_forward(x, Win, conv_w, conv_b, Wx, A_log, D, Wout, ln_g, ln_b)

    def _L0_ffn_ref(x, weight):
        import jax, jax.numpy as jnp
        import numpy as np
        w_bin = jnp.sign(weight)
        return jnp.einsum('bsi,oi->bso', x, w_bin)

    def _L1_attn_ref(x, ln_g, ln_b, W_in, b_in, W_conv, b_conv, W_xp, b_xp, W_dt, b_dt, W_us, b_us, W_out, b_out):
        import jax, jax.numpy as jnp
        import numpy as np
        B, L, D_MODEL = (2, 1024, 192)
        D_STATE, D_CONV, EXPAND = (16, 4, 2)
        E = EXPAND * D_MODEL
        LN_EPS = 1e-05
        Bsz, Ls, Dm = x.shape
        mu = jnp.mean(x, axis=-1, keepdims=True)
        var = jnp.mean((x - mu) ** 2, axis=-1, keepdims=True)
        xn = (x - mu) * jax.lax.rsqrt(var + LN_EPS) * ln_g + ln_b
        x_in = xn @ W_in + b_in
        xc = jnp.transpose(x_in, (0, 2, 1))
        xc = jax.lax.conv_general_dilated(xc, W_conv, window_strides=(1,), padding=[(D_CONV - 1, 0)], dimension_numbers=('NCH', 'OIH', 'NCH'), feature_group_count=E) + b_conv[None, :, None]
        x_act = jax.nn.silu((jnpp := jnp.transpose(xc, (0, 2, 1))))
        xd = x_act @ W_xp + b_xp
        xs, ds = (xd[..., :Dm], xd[..., Dm:])
        dt = jax.nn.softplus(x_act @ W_dt + b_dt)
        a = jnp.exp(-dt)
        bterm = ds * jnp.exp(-dt / 2)

        def step(carry, ab):
            at, bt = ab
            v = at * carry + bt
            return (v, v)
        _, v = jax.lax.scan(step, jnp.zeros((Bsz, dt.shape[-1]), x.dtype), (jnp.swapaxes(a, 0, 1), jnp.swapaxes(bterm, 0, 1)))
        v = jnp.swapaxes(v, 0, 1)
        k = jnp.arange(Ls - 1, -1, -1, dtype=x.dtype)[None, :, None]
        denom = jnp.expm1(-dt)
        denom = jnp.where(denom > -1e-30, -1e-30, denom)
        us = jnp.exp(-k * dt) * v + bterm * jnp.expm1(-k * dt) / denom
        y = xs + us @ W_us + b_us
        y = jnp.concatenate([y, x_act[..., Dm:]], axis=-1) @ W_out + b_out
        return y

    def _L1_ffn_ref(x, gate_weight, gate_bias, w1, w2, w3, sw1, sw2, sw3):
        import jax, jax.numpy as jnp
        import numpy as np
        from jax import lax
        DIM = 192
        INTER = 128
        E = 8
        G = 4
        TOPK_G = 2
        TOPK = 2
        ROUTE_SCALE = 1.0

        def _gate(x2, gate_weight, gate_bias):
            T = x2.shape[0]
            scores = jax.nn.sigmoid(x2 @ gate_weight.T)
            s = scores + gate_bias
            sv = s.reshape(T, G, E // G)
            top2, _ = lax.top_k(sv, 2)
            group_scores = top2.sum(-1)
            _, gidx = lax.top_k(group_scores, TOPK_G)
            gmask = jnp.zeros((T, G), bool).at[jnp.arange(T)[:, None], gidx].set(True)
            masked = jnp.where(gmask[:, :, None], sv, -jnp.inf).reshape(T, E)
            _, idx = lax.top_k(masked, TOPK)
            w = jnp.take_along_axis(scores, idx, axis=1)
            w = w / (w.sum(-1, keepdims=True) + 1e-06) * ROUTE_SCALE
            return (w, idx)
        B, S, D = x.shape
        x2 = x.reshape(-1, D)
        T = x2.shape[0]
        weights, indices = _gate(x2, gate_weight, gate_bias)
        cw = jnp.zeros((T, E), x.dtype).at[jnp.arange(T)[:, None], indices].add(weights)
        h1 = jnp.einsum('td,eid->tei', x2, w1)
        h3 = jnp.einsum('td,eid->tei', x2, w3)
        h = jax.nn.silu(h1) * h3
        y = jnp.einsum('tei,edi,te->td', h, w2, cw)
        z = jax.nn.silu(x2 @ sw1.T) * (x2 @ sw3.T) @ sw2.T
        return (y + z).reshape(B, S, D)
    h = _L0_tok_ref(x, L0_tok_curve, L0_tok_proj_w, L0_tok_proj_b)
    h = _layernorm(h + _L0_attn_ref(h, L0_attn_Win, L0_attn_conv_w, L0_attn_conv_b, L0_attn_Wx, L0_attn_A_log, L0_attn_D, L0_attn_Wout, L0_attn_ln_g, L0_attn_ln_b), axis=-1)
    h = _layernorm(h + _L0_ffn_ref(h, L0_ffn_weight), axis=-1)
    h = _layernorm(h + _L1_attn_ref(h, L1_attn_ln_g, L1_attn_ln_b, L1_attn_W_in, L1_attn_b_in, L1_attn_W_conv, L1_attn_b_conv, L1_attn_W_xp, L1_attn_b_xp, L1_attn_W_dt, L1_attn_b_dt, L1_attn_W_us, L1_attn_b_us, L1_attn_W_out, L1_attn_b_out), axis=-1)
    h = _layernorm(h + _L1_ffn_ref(h, L1_ffn_gate_weight, L1_ffn_gate_bias, L1_ffn_w1, L1_ffn_w2, L1_ffn_w3, L1_ffn_sw1, L1_ffn_sw2, L1_ffn_sw3), axis=-1)
    return h

_drawn_inputs = setup_inputs


def setup_inputs(seed=0):
    import zlib

    import numpy as np

    out = dict(_drawn_inputs(seed))
    spreads = {'L0_attn_conv_b': (0.0, 0.1),
     'L0_attn_D': (1.0, 0.6),
     'L0_attn_ln_g': (1.0, 0.6),
     'L0_attn_ln_b': (0.0, 0.8),
     'L1_attn_ln_g': (1.0, 0.6),
     'L1_attn_ln_b': (0.0, 0.8),
     'L1_attn_b_in': (0.0, 0.8),
     'L1_attn_b_conv': (0.0, 0.531),
     'L1_attn_b_xp': (0.0, 0.276),
     'L1_attn_b_dt': (0.0, 0.8),
     'L1_attn_b_us': (0.0, 0.8),
     'L1_attn_b_out': (0.0, 0.8),
     'L1_ffn_gate_bias': (0.0, 0.1)}
    factors = {'L0_attn_conv_w': 6.95,
     'L0_attn_Wx': 8.0,
     'L0_attn_A_log': 30.722,
     'L1_attn_W_in': 5.798,
     'L1_attn_W_conv': 5.264,
     'L1_attn_W_xp': 7.348,
     'L1_attn_W_dt': 8.0,
     'L1_attn_W_us': 8.0}
    for name, (base, spread) in spreads.items():
        noise = np.random.default_rng([zlib.crc32(name.encode()), seed]).standard_normal(out[name].shape)
        drawn = base * np.exp(spread * noise) if base else spread * noise
        out[name] = jnp.asarray(drawn.astype(out[name].dtype))
    for name, factor in factors.items():
        out[name] = (out[name] * factor).astype(out[name].dtype)
    return out
```

```python
import concourse.bass as bass
from concourse import mybir
from contextlib import ExitStack
import numpy as np

F32, BF16, I32 = mybir.dt.float32, mybir.dt.bfloat16, mybir.dt.int32
ALU, ACT, AX = mybir.AluOpType, mybir.ActivationFunctionType, mybir.AxisListType

IMAGES, CH, SIDE = 64, 3, 112
L, DM, DI, DS = 256, 192, 384, 32
TAPS0, TAPS1, N16 = 7, 4, 16
E, INTER = 8, 128
PAIR = 2
TOK = PAIR * L
UNITS = IMAGES // PAIR
TILES = TOK // 128
KC, KM = 96, DM // 96
CI = DI // 128
NG = 2
GROUPS = DS // NG
BLOCKS = GROUPS * CI
NA, NX = 2, 3
LAG = 1
ROUTE_OPS, SETUP_DVE, SETUP_ACT = 29, 16, 2
LOG_MAX = 88.0
PAD = TAPS0 - 1
EPS = 1e-5
BIG = 3.0e38


def columns(widths):
    at, start = {}, 0
    for name, w in widths:
        at[name] = (start, w)
        start += w
    return at, start


W128, N128 = columns([
    ("ident", 128), ("wx_bc", CI * 192), ("wx_d", CI * DI), ("wout", CI * DM), ("wo_x", 2 * DM),
    ("wxp", CI * DM), ("wsd", CI * 48), ("w2", (E + 1) * DM), ("a_log", CI * DS), ("cw0", CI * TAPS0),
    ("cb0", CI), ("dskip", CI), ("b_in", CI), ("cw1", CI * TAPS1), ("cb1", CI), ("part", 1), ("m1", 1),
    ("m2", 1), ("pw", CH * DM), ("pb", DM), ("gbias", E), ("ones", 128), ("b_out", DM), ("b_dt", 1),
    ("b_ds", 1), ("k", L), ("w_us", DM), ("lt4", 16), ("lt8", 64), ("half", TILES), ("eps", TILES)])
W96, N96 = columns([
    ("win", KM * 2 * DI), ("ffn", KM * DM), ("w_in", KM * DI), ("wo_y", KM * DM), ("gate", KM * E),
    ("w1", KM * (E + 1) * INTER), ("w3", KM * (E + 1) * INTER), ("g0", KM), ("b0", KM), ("g1", KM),
    ("b1", KM), ("by1", KM), ("by2", KM)])

FIRST_SIDE = 3
POST = [["outproj", "res1"], ["norm1"], ["x1T"], ["ffn", "res2"], ["norm2"], ["prenorm"], ["xnT"],
        ["w_in", "conv1"], ["gate1"], ["xd", "dt"], ["decay", "states"], ["y1"], ["w_out", "res3"], ["norm3"],
        ["x3T"], ["gate", "route"], ["cwT"]] + [[f"expert{e}"] for e in range(E + 1)] + [["experts_end"], ["norm4"]]
PRE = [["gather"], ["embed"], ["norm0"], ["x0T"], ["xz0"], ["xz1"], ["xz2"], ["xc_end"], ["bc"], ["bc_low"],
       ["delta0"], ["delta1"], ["delta2"]]
PLAN = {b: [] for b in range(BLOCKS)}
for _n, _row in enumerate([("post", r) for r in POST] + [("pre", r) for r in PRE]):
    PLAN[FIRST_SIDE + _n] = [(_row[0], s) for s in _row[1]]
TAIL_BLOCK = 2


class Unit:

    def __init__(self, n, parity):
        self.n, self.parity = n, parity
        self.has_previous = not isinstance(n, int) or n > 0

    def nth(self, per_unit, k):
        return self.n * per_unit + k

    def before(self, per_unit, k):
        return self.n * per_unit + (k - per_unit)


def build(nc, x, curve, p128, p96, sel, sel_e, out, units=UNITS):
    ctx = ExitStack()
    with ctx:
        def sb(name, shape, dt=F32):
            return ctx.enter_context(nc.sbuf_tensor(name, shape, dt))

        def sem(name):
            return ctx.enter_context(nc.semaphore(name))

        w128, w96 = sb("w128", [128, N128]), sb("w96", [KC, N96])
        sel_sb, sel_e_sb = sb("sel_sb", [96, DS, 128], BF16), sb("sel_e_sb", [3 * E, E, 128], BF16)
        row_hot, col_hot = sb("row_hot", [SIDE, L]), sb("col_hot", [SIDE, L])
        diag_d = sb("diag_d", [128, CI, 128])

        def p(name, rows=128, **dims):
            a, w = W128[name]
            v = w128[0:rows, a:a + w]
            return v.rearrange("p (a b) -> p a b", **dims) if dims else v

        def q(name, **dims):
            a, w = W96[name]
            v = w96[:, a:a + w]
            return v.rearrange("p (a b) -> p a b", **dims) if dims else v

        ident = p("ident")
        wx_bc, wx_d, wout = p("wx_bc", a=CI), p("wx_d", a=CI), p("wout", a=CI)
        wo_x, wxp, wsd, w2 = p("wo_x", a=2), p("wxp", a=CI), p("wsd", a=CI), p("w2", a=E + 1)
        a_neg, cw0, cb0, dskip = p("a_log", a=CI), p("cw0", a=CI), p("cb0"), p("dskip")
        b_in, cw1, cb1, part = p("b_in"), p("cw1", a=CI), p("cb1"), p("part", SIDE)
        m1, m2, pw, pb = p("m1", 96), p("m2", 96), p("pw", SIDE, a=CH), p("pb")
        gbias, ones, b_out, b_dt, b_ds = p("gbias"), p("ones", 1), p("b_out", 1), p("b_dt", N16), p("b_ds")
        ktab, w_us, lt4, lt8, half, eps = p("k", N16), p("w_us", N16), p("lt4", a=4), p("lt8", a=8), p("half"), p("eps")
        win, ffn_w, w_in, wo_y = q("win", a=KM), q("ffn", a=KM), q("w_in", a=KM), q("wo_y", a=KM)
        gate_w, w1, w3 = q("gate", a=KM), q("w1", a=KM), q("w3", a=KM)
        g0, b0, g1, b1, by1, by2 = (q(n) for n in ("g0", "b0", "g1", "b1", "by1", "by2"))

        decay = sb("decay", [128, NA, NG, TOK])
        drive = sb("drive", [128, NX, NG, TOK])
        bc_rep = sb("bc_rep", [128, 2, 2, NG, TOK])
        delta, du, gz = (sb(n, [128, 2, CI, TOK]) for n in ("delta", "du", "gz"))
        bc_st = sb("bc_st", [96, 2, 2, TOK], BF16)
        xc = sb("xc", [128, CI, TOK])
        h0 = sb("h0", [128, 2, TILES, DM])
        img = sb("img", [SIDE, PAIR * CH, SIDE])
        xs = sb("xs", [128, TILES, DM])
        xn = sb("xn", [128, TILES, DM])
        xT = sb("xT", [KC, KM, TOK])
        convin = sb("convin", [128, CI, PAIR, PAD + L])
        act1 = sb("act1", [128, CI, TOK])
        th = sb("th", [128, 3, TOK])
        stats, mv, rstd = sb("stats", [128, TILES, 6]), sb("mv", [128, TILES, 2]), sb("rstd", [128, TILES])
        spare = sb("spare", [128, 1])
        S = sb("S", [128, 7, TOK])
        gt_ = sb("gt_", [128, 308])
        cwT = sb("cwT", [3 * E, TOK], BF16)
        hb = sb("hb", [128, TILES * E], BF16)
        curve_i = S[0:SIDE, 0, :].bitcast(I32).rearrange("p (a n) -> p a n", a=2)
        masked = S[0:SIDE, 0:3, :]
        low, hi16 = S[0:96, 0:2, :], S[0:96, 2, :].bitcast(BF16).rearrange("p (a t) -> p a t", a=2)
        soft = S[:, 3:7, :].rearrange("p (r a) t -> p r a t", a=2)
        s_x, s_e, s_dt, s_ds, s_k, s_p, s_v = (S[0:N16, i, :] for i in range(7))
        s_t, s_az = th[0:N16, 0, :], th[0:N16, 1, :]
        y1T = xT
        r_score, r_s, r_m, r_sel, r_cw = (gt_[:, TILES * E * i:TILES * E * (i + 1)] for i in range(5))
        r_g, r_gsel, r_off = (gt_[:, 160 + 16 * i:176 + 16 * i] for i in range(3))
        r_sum, cws = gt_[:, 208:212], gt_[:, 212:308].rearrange("p (k e) -> p k e", e=3 * E)
        r_gt, r_eq = S[:, 0, 0:TILES * E * E], S[:, 1, 0:TILES * E * E]
        hid, crep = S[:, 2:4, :], S[:, 4:6, :]

        y = [ctx.enter_context(nc.psum_tensor(f"y{c}", [128, TOK], F32)) for c in range(CI)]
        rep = ctx.enter_context(nc.psum_tensor("rep", [128, TOK], F32))
        T = [ctx.enter_context(nc.psum_tensor(f"T{c}", [128, TOK], F32)) for c in range(4)]

        def two(bank):
            return T[bank][:, 0:2 * DM].rearrange("p (a d) -> p a d", a=2)

        class Signal:
            def __init__(self, name, per_unit, step=1):
                self.sem, self.per_unit, self.step = sem(name), per_unit * step, step

            def of(self, unit, k=None):
                return self.sem, unit.nth(self.per_unit, self.per_unit if k is None else k * self.step)

            def before(self, unit):
                return self.sem, unit.nth(self.per_unit, 0)

        loaded, setup_act, setup_dve = sem("loaded"), sem("setup_act"), sem("setup_dve")
        img_in = Signal("img_in", 1, 16)
        out_done = Signal("out_done", 1, 16)
        rep_mm = Signal("rep_mm", 4 * GROUPS)
        rep_out = Signal("rep_out", 4 * GROUPS)
        decay_ready = Signal("decay_ready", BLOCKS)
        drive_dve = Signal("drive_dve", BLOCKS - GROUPS)
        drive_pool = Signal("drive_pool", GROUPS)
        scanned = Signal("scanned", BLOCKS)
        weighted = Signal("weighted", BLOCKS)
        summed = Signal("summed", BLOCKS)
        diag_in = Signal("diag_in", CI)
        gated = Signal("gated", CI)
        post_stats = Signal("post_stats", 5 * 2 * TILES)
        post_rstd = Signal("post_rstd", 5 * 2)
        post_norm = Signal("post_norm", 5 * TILES)
        pre_stats, pre_rstd, pre_norm = Signal("pre_stats", 2 * TILES), Signal("pre_rstd", 2), Signal("pre_norm", TILES)
        post_tp, post_xT = Signal("post_tp", 3 * KM), Signal("post_xT", 3 * KM)
        pre_tp, pre_xT = Signal("pre_tp", KM), Signal("pre_xT", KM)
        outproj_pe, ffn_pe, w_out_pe = Signal("outproj_pe", 2), Signal("ffn_pe", 2), Signal("w_out_pe", 2)
        res_dve = Signal("res_dve", 4 * 2)
        w_in_pe, w_in_act = Signal("w_in_pe", CI), Signal("w_in_act", CI)
        conv1_dve, conv1_act = Signal("conv1_dve", CI * (TAPS1 + 1)), Signal("conv1_act", CI)
        xd_pe, xd_act, dt_dve = Signal("xd_pe", 1), Signal("xd_act", 5), Signal("dt_dve", 4)
        decay_act, states_dve = Signal("decay_act", 6), Signal("states_dve", 10)
        y1_pe, y1_act = Signal("y1_pe", KM), Signal("y1_act", KM)
        gate_pe, gate_act, route_dve = Signal("gate_pe", 1), Signal("gate_act", 1), Signal("route_dve", ROUTE_OPS)
        cwT_pe, cwT_act = Signal("cwT_pe", 1), Signal("cwT_act", 1)
        expert_up = Signal("expert_up", 2 * (E + 1))
        expert_tanh = Signal("expert_tanh", E + 1)
        expert_hid = Signal("expert_hid", 2 * (E + 1))
        crep_mm, crep_out = Signal("crep_mm", E), Signal("crep_out", E)
        expert_scaled = Signal("expert_scaled", E)
        expert_down = Signal("expert_down", E + 1)
        gather_pe, gather_dve = Signal("gather_pe", CH), Signal("gather_dve", CH)
        embed_pe, embed_dve = Signal("embed_pe", 2), Signal("embed_dve", 2)
        xz_pe, xz_act = Signal("xz_pe", 2 * CI), Signal("xz_act", 3 * CI)
        xz_dve = Signal("xz_dve", (TAPS0 + 2) * CI)
        bc_pe, bc_act, bc_dve = Signal("bc_pe", 2), Signal("bc_act", 4), Signal("bc_dve", 4)
        delta_pe, delta_act = Signal("delta_pe", CI), Signal("delta_act", 3 * CI)
        delta_dve, delta_pool = Signal("delta_dve", 2 * CI), Signal("delta_pool", CI)

        block = ctx.enter_context(nc.Block())

        def run_units(eng, prologue, body, epilogue):
            prologue(Unit(0, 0))

            def one(n, parity):
                body(Unit(n, parity), Unit(n - 1, 1 - parity) if not isinstance(n, int) or n > 0 else None,
                     Unit(n + 1, 1 - parity) if not isinstance(n, int) or n < units - 1 else None)

            one(0, 0)
            one(1, 1)
            if units > 4:
                with eng.Fori(1, units // 2 - 1) as j:
                    one(j * 2, 0)
                    one(j * 2 + 1, 1)
            if units > 2:
                one(units - 2, 0)
                one(units - 1, 1)
            epilogue(Unit(units - 1, 1))

        def halves(ap):
            return ap.rearrange("p (b t) -> p b t", b=PAIR)

        def twice(ap):
            return ap.unsqueeze(1).broadcast_to([ap.shape[0], PAIR, L])

        def on_pool(b):
            return b % CI == 1

        def drives(b):
            pool = sum(on_pool(i) for i in range(b + 1))
            return b + 1 - pool, pool

        def rep_jobs(b):
            return [(i // NG, i % NG) for i in ((0, 1), (2,), (3,))[b % CI]]

        def rep_target(U, W, b):
            g = b // CI + 1
            return (U, g) if g < GROUPS else (W, 0)

        @block.sync
        def _(sp):
            sp.dma_start(w128[:, :], p128).then_inc(loaded, 16)
            sp.dma_start(w96[:, :], p96).then_inc(loaded, 16)
            sp.dma_start(sel_sb[:, :, :], sel.rearrange("p (n m) -> p n m", n=DS)).then_inc(loaded, 16)
            sp.dma_start(sel_e_sb[:, :, :], sel_e.rearrange("p (n m) -> p n m", n=E)).then_inc(loaded, 16)
            sp.dma_start(curve_i[:, :, :],
                         curve.rearrange("(a c) n -> a c n", a=1).broadcast_to([SIDE, 2, L])).then_inc(loaded, 16)

            def load_images(W):
                if W.has_previous:
                    sp.wait_ge(*gather_pe.before(W))
                sp.dma_start(img[:, :, :], x[bass.ds(W.n * (PAIR * CH), PAIR * CH), :, :].rearrange(
                    "c h w -> h c w")).then_inc(img_in.sem, 16)

            def store(V):
                sp.wait_ge(*post_norm.of(V))
                sp.dma_start(out[bass.ds(V.n * TOK, TOK), :].rearrange("(k p) d -> p k d", p=128),
                             xs[:, :, :]).then_inc(out_done.sem, 16)

            def body(U, V, W):
                if W:
                    load_images(W)
                if V:
                    store(V)

            run_units(sp, load_images, body, store)
            sp.wait_ge(out_done.sem, 16 * units)

        @block.tensor
        def _(pe):
            mm = nc.tensor.matmul
            rep_reader = [None]

            def transposes(src, banks, done):
                for c in range(KM):
                    for k in range(TILES):
                        last = nc.tensor.transpose(T[banks[c]][0:KC, k * 128:(k + 1) * 128],
                                                   src[:, k, c * KC:(c + 1) * KC], ident)
                    last.then_inc(done.sem, 1)

            def token_major(dst, k, pairs, signal):
                for n, (lhs, rhs) in enumerate(pairs):
                    last = mm(dst[:, k % 2, :], lhs, rhs, start=(n == 0), stop=(n == len(pairs) - 1))
                if k % 2:
                    last.then_inc(signal.sem, 1)

            def tok(k):
                return slice(k * 128, (k + 1) * 128)

            def outproj(V):
                pe.wait_ge(*gated.of(V))
                for k in range(TILES):
                    token_major(two(k // 2), k, [(act1[:, c, tok(k)], wout[:, c, :]) for c in range(CI)], outproj_pe)

            def post_transpose(n, src, norm):
                def step(V):
                    pe.wait_ge(*post_norm.of(V, TILES * norm))
                    transposes(src, (2, 3), post_tp)
                return step

            def ffn(V):
                pe.wait_ge(*post_xT.of(V, KM))
                for k in range(TILES):
                    token_major(two(k // 2), k, [(xT[:, c, tok(k)], ffn_w[:, c, :]) for c in range(KM)], ffn_pe)

            def w_in_step(V):
                pe.wait_ge(*post_xT.of(V, 2 * KM))
                for m in range(CI):
                    for c in range(KM):
                        last = mm(T[m][:, :], w_in[:, c, m * 128:(m + 1) * 128], xT[:, c, :],
                                  start=(c == 0), stop=(c == KM - 1))
                    last.then_inc(w_in_pe.sem, 1)

            def xd(V):
                pe.wait_ge(*conv1_dve.of(V))
                for c in range(CI):
                    last = mm(T[3][0:48, :], wsd[:, c, :], act1[:, c, :], start=(c == 0), stop=(c == CI - 1))
                last.then_inc(xd_pe.sem, 1)
                for half_ in range(KM):
                    for c in range(CI):
                        mm(T[half_][0:KC, :], wxp[:, c, half_ * KC:(half_ + 1) * KC], act1[:, c, :],
                           start=(c == 0), stop=False, skip_group_check=True)

            def y1(V):
                pe.wait_ge(*states_dve.of(V))
                for half_ in range(KM):
                    mm(T[half_][0:KC, :], w_us[:, half_ * KC:(half_ + 1) * KC], s_v,
                       start=False, stop=True, skip_group_check=True).then_inc(y1_pe.sem, 1)

            def w_out(V):
                pe.wait_ge(*y1_act.of(V))
                for k in range(TILES):
                    token_major(two(2 + k // 2), k,
                                [(y1T[:, c, tok(k)], wo_y[:, c, :]) for c in range(KM)] +
                                [(act1[:, 1 + c, tok(k)], wo_x[:, c, :]) for c in range(2)] +
                                [(ones, b_out)], w_out_pe)

            def gate(V):
                pe.wait_ge(*post_xT.of(V))
                for k in range(TILES):
                    for c in range(KM):
                        last = mm(T[0][:, k * E:(k + 1) * E], xT[:, c, tok(k)], gate_w[:, c, :],
                                  start=(c == 0), stop=(c == KM - 1))
                last.then_inc(gate_pe.sem, 1)

            def cw_transpose(V):
                pe.wait_ge(*route_dve.of(V))
                for k in range(TILES):
                    last = nc.tensor.transpose(T[0][0:3 * E, tok(k)], cws[:, k, :], ident)
                last.then_inc(cwT_pe.sem, 1)

            def down(V, e):
                if e < E:
                    pe.wait_ge(*expert_scaled.of(V, e + 1))
                else:
                    pe.wait_ge(*expert_hid.of(V))
                for k in range(TILES):
                    last = mm(two(2 + k // 2)[:, k % 2, :], hid[:, e % 2, tok(k)], w2[:, e, :],
                              start=(e == 0 and k % 2 == 0), stop=(e == E), skip_group_check=True)
                last.then_inc(expert_down.sem, 1)

            def expert(e):
                def step(V, U, b):
                    if e == 0:
                        pe.wait_ge(*cwT_act.of(V))
                    else:
                        pe.wait_ge(*expert_hid.of(V, 2 * e - 1))
                    for i, w in ((0, w1), (1, w3)):
                        if i and e:
                            pe.wait_ge(*expert_hid.of(V, 2 * e))
                        for c in range(KM):
                            last = mm(T[i][:, :], w[:, c, e * INTER:(e + 1) * INTER], xT[:, c, :],
                                      start=(c == 0), stop=(c == KM - 1))
                        last.then_inc(expert_up.sem, 1)
                    if e < E:
                        if rep_reader[0]:
                            pe.wait_ge(*rep_reader[0])
                        elif U:
                            pe.wait_ge(*rep_out.of(*rep_done(U, b)))
                        mm(rep[:, :], sel_e_sb[:, e, :], cwT[:, :], start=True, stop=True).then_inc(crep_mm.sem, 1)
                        rep_reader[0] = crep_out.of(V, e + 1)
                    if e:
                        down(V, e - 1)
                return step

            def experts_end(V):
                down(V, E)

            def gather(W, V):
                pe.wait_ge(*img_in.of(W))
                if W.has_previous:
                    pe.wait_ge(*delta_dve.before(W))
                if V:
                    pe.wait_ge(*res_dve.of(V))
                for ch in range(CH):
                    for b in range(PAIR):
                        last = mm(T[ch][0:SIDE, b * L:(b + 1) * L], img[:, b * CH + ch, :], row_hot[:, :],
                                  start=True, stop=True)
                    last.then_inc(gather_pe.sem, 1)

            def embed(W):
                pe.wait_ge(*gather_dve.of(W))
                for k in range(TILES):
                    token_major(two((3, 0)[k // 2]), k, [(masked[:, ch, tok(k)], pw[:, ch, :]) for ch in range(CH)],
                                embed_pe)

            def x0T(W):
                pe.wait_ge(*pre_norm.of(W))
                transposes(xn, (2, 3), pre_tp)

            def xz(m):
                def step(W):
                    if m == 0:
                        pe.wait_ge(*pre_xT.of(W))
                    else:
                        pe.wait_ge(*xz_act.of(W, 3 * m - 1))
                        pe.wait_ge(*xz_dve.of(W, 9 * m - 1))
                    for i in range(2):
                        for c in range(KM):
                            last = mm(T[i][:, :], win[:, c, i * DI + m * 128:i * DI + (m + 1) * 128], xT[:, c, :],
                                      start=(c == 0), stop=(c == KM - 1))
                        last.then_inc(xz_pe.sem, 1)
                return step

            def bc(W):
                pe.wait_ge(*xz_dve.of(W))
                for i in range(2):
                    for c in range(CI):
                        last = mm(T[i][0:96, :], wx_bc[:, c, i * 96:(i + 1) * 96], xc[:, c, :],
                                  start=(c == 0), stop=(c == CI - 1))
                    last.then_inc(bc_pe.sem, 1)

            def delta_step(m):
                def step(W):
                    if m == 2:
                        pe.wait_ge(*bc_dve.of(W, 2))
                    bank = (2, 3, 0)[m]
                    for c in range(CI):
                        last = mm(T[bank][:, :], wx_d[:, c, m * 128:(m + 1) * 128], xc[:, c, :],
                                  start=(c == 0), stop=(c == CI - 1))
                    last.then_inc(delta_pe.sem, 1)
                return step

            post = {"outproj": outproj, "x1T": post_transpose(0, xs, 1), "ffn": ffn, "xnT": post_transpose(1, xn, 3),
                    "w_in": w_in_step, "xd": xd, "y1": y1, "w_out": w_out, "x3T": post_transpose(2, xs, 4),
                    "gate": gate, "cwT": cw_transpose, "experts_end": experts_end}
            experts = {f"expert{e}": expert(e) for e in range(E + 1)}
            pre = {"embed": embed, "x0T": x0T, "xz0": xz(0), "xz1": xz(1), "xz2": xz(2), "bc": bc,
                   "delta0": delta_step(0), "delta1": delta_step(1), "delta2": delta_step(2)}

            def replicate(unit, g, i, s):
                n = 4 * g + 2 * i + s
                if n == 0:
                    pe.wait_ge(*bc_dve.of(unit))
                if rep_reader[0]:
                    pe.wait_ge(*rep_reader[0])
                    rep_reader[0] = None
                elif n or unit.has_previous:
                    pe.wait_ge(*rep_out.of(unit, n))
                mm(rep[:, :], sel_sb[:, NG * g + s, :], bc_st[:, unit.parity, i, :], start=True,
                   stop=True).then_inc(rep_mm.sem, 1)

            def rep_done(U, b):
                return U, 4 * (b // CI + 1) + (0, 2, 3)[b % CI]

            def add_up(U, b):
                g, c = b // CI, b % CI
                if g == 0:
                    if U.has_previous:
                        pe.wait_ge(*gated.before(U))
                    mm(y[c][:, :], diag_d[:, c, :], xc[:, c, :], start=True, stop=False,
                       skip_group_check=True).then_inc(diag_in.sem, 1)
                pe.wait_ge(*weighted.of(U, b + 1))
                for s in range(NG):
                    last = mm(y[c][:, :], ident, drive[:, b % NX, s, :], start=False,
                              stop=(g == GROUPS - 1 and s == NG - 1), skip_group_check=True)
                last.then_inc(summed.sem, 1)

            def first_group(W):
                for i in range(2):
                    for s in range(NG):
                        replicate(W, 0, i, s)

            def prologue(W):
                pe.wait_ge(setup_dve, SETUP_DVE)
                pe.wait_ge(setup_act, SETUP_ACT)
                pe.wait_ge(loaded, 5 * 16)
                gather(W, None)
                for s in sum(PRE, []):
                    if s in pre:
                        pre[s](W)
                first_group(W)

            def side(kind, s, U, V, W, b):
                if kind == "post" and V:
                    if s in experts:
                        experts[s](V, U, b)
                    elif s in post:
                        post[s](V)
                if kind == "pre" and W:
                    if s == "gather":
                        gather(W, V)
                    elif s in pre:
                        pre[s](W)

            def body(U, V, W):
                for b in range(BLOCKS):
                    for kind, s in PLAN[b]:
                        side(kind, s, U, V, W, b)
                    unit, g = rep_target(U, W, b)
                    if unit:
                        for i, s in rep_jobs(b):
                            replicate(unit, g, i, s)
                    if b >= LAG:
                        add_up(U, b - LAG)
                    elif V:
                        add_up(V, BLOCKS + b - LAG)

            def epilogue(V):
                for b in range(BLOCKS - LAG, BLOCKS):
                    add_up(V, b)
                rep_reader[0] = rep_out.of(V)
                for s in sum(POST, []):
                    side("post", s, None, V, None, 0)

            run_units(pe, prologue, body, epilogue)

        @block.scalar
        def _(act):
            f = nc.scalar.activation

            def post_evacuate(n, scale=None, bias=None):
                def step(V):
                    for c in range(KM):
                        act.wait_ge(*post_tp.of(V, KM * n + c + 1))
                        if scale is None:
                            f(xT[:, c, :], T[2 + c][0:KC, :], ACT.Copy).then_inc(post_xT.sem, 1)
                        else:
                            f(xT[:, c, :], T[2 + c][0:KC, :], ACT.Identity, scale=scale[:, c:c + 1],
                              bias=bias[:, c:c + 1]).then_inc(post_xT.sem, 1)
                return step

            def w_in_step(V):
                for m in range(CI):
                    act.wait_ge(*w_in_pe.of(V, m + 1))
                    f(convin[:, m, :, PAD:], halves(T[m][:, :]), ACT.Identity,
                      bias=b_in[:, m:m + 1]).then_inc(w_in_act.sem, 1)

            def conv1(V):
                for m in range(CI):
                    act.wait_ge(*conv1_dve.of(V, CI * (TAPS1 - 1) + m + 1))
                    f(th[:, m, :], act1[:, m, :], ACT.Tanh).then_inc(conv1_act.sem, 1)

            def xd(V):
                act.wait_ge(*xd_pe.of(V))
                f(s_e, T[3][0:N16, :], ACT.Abs, bias=b_dt).then_inc(xd_act.sem, 1)
                f(s_x, T[3][0:N16, :], ACT.Identity, bias=b_dt).then_inc(xd_act.sem, 1)
                f(s_ds, T[3][32:48, :], ACT.Identity, bias=b_ds[32:48, :]).then_inc(xd_act.sem, 1)
                act.wait_ge(*xd_act.of(V, 1))
                f(s_e, s_e, ACT.Exp, scale=-1.0).then_inc(xd_act.sem, 1)
                act.wait_ge(*xd_act.of(V, 4))
                f(s_dt, s_e, ACT.Ln, bias=1.0).then_inc(xd_act.sem, 1)

            def decay_step(V):
                act.wait_ge(*dt_dve.of(V, 3))
                f(s_x, s_dt, ACT.Exp, scale=-1.0).then_inc(decay_act.sem, 1)
                f(halves(s_az)[:, :, 1:], halves(s_dt)[:, :, 1:], ACT.Exp, scale=-1.0).then_inc(decay_act.sem, 1)
                f(s_e, s_dt, ACT.Exp, scale=-0.5).then_inc(decay_act.sem, 1)
                act.wait_ge(*dt_dve.of(V))
                f(s_p, s_k, ACT.Exp, scale=-1.0).then_inc(decay_act.sem, 1)
                f(s_t, s_dt, ACT.Tanh, scale=0.5).then_inc(decay_act.sem, 1)
                f(s_k, s_k, ACT.Tanh, scale=0.5).then_inc(decay_act.sem, 1)

            def y1(V):
                for c in range(KM):
                    act.wait_ge(*y1_pe.of(V, c + 1))
                    f(y1T[:, c, :], T[c][0:KC, :], ACT.Identity, bias=by1[:, c:c + 1]).then_inc(y1_act.sem, 1)

            def gate(V):
                act.wait_ge(*gate_pe.of(V))
                f(r_score, T[0][:, 0:TILES * E], ACT.Tanh, scale=0.5).then_inc(gate_act.sem, 1)

            def cw_transpose(V):
                act.wait_ge(*cwT_pe.of(V))
                f(cwT[:, :], T[0][0:3 * E, :], ACT.Copy).then_inc(cwT_act.sem, 1)

            def expert(e):
                def step(V):
                    act.wait_ge(*expert_up.of(V, 2 * e + 1))
                    f(th[:, e % 3, :], T[0][:, :], ACT.Tanh).then_inc(expert_tanh.sem, 1)
                    if e < E:
                        act.wait_ge(*crep_mm.of(V, e + 1))
                        if e >= 2:
                            act.wait_ge(*expert_scaled.of(V, e - 1))
                        f(crep[:, e % 2, :], rep[:, :], ACT.Copy).then_inc(crep_out.sem, 1)
                return step

            def x0T(W):
                for c in range(KM):
                    act.wait_ge(*pre_tp.of(W, c + 1))
                    f(xT[:, c, :], T[2 + c][0:KC, :], ACT.Identity, scale=g0[:, c:c + 1],
                      bias=b0[:, c:c + 1]).then_inc(pre_xT.sem, 1)

            def tanh_xc(W, m):
                act.wait_ge(*xz_dve.of(W, 9 * m + TAPS0))
                f(th[:, 1, :], xc[:, m, :], ACT.Tanh).then_inc(xz_act.sem, 1)

            def xz(m):
                def step(W):
                    act.wait_ge(*xz_pe.of(W, 2 * m + 1))
                    f(convin[:, m, :, PAD:], halves(T[0][:, :]), ACT.Copy).then_inc(xz_act.sem, 1)
                    act.wait_ge(*xz_pe.of(W, 2 * m + 2))
                    f(th[:, 0, :], T[1][:, :], ACT.Tanh).then_inc(xz_act.sem, 1)
                    tanh_xc(W, m)
                return step

            def bc(W):
                for i in range(2):
                    act.wait_ge(*bc_pe.of(W, i + 1))
                    f(hi16[:, i, :], T[i][0:96, :], ACT.Copy).then_inc(bc_act.sem, 1)

            def bc_low(W):
                for i in range(2):
                    act.wait_ge(*bc_dve.of(W, i + 1))
                    f(hi16[:, i, :], low[:, i, :], ACT.Copy).then_inc(bc_act.sem, 1)

            def delta_step(m):
                def step(W):
                    bank, r = (2, 3, 0)[m], m % 2
                    act.wait_ge(*delta_pe.of(W, m + 1))
                    if m == 2:
                        act.wait_ge(*delta_dve.of(W, 2))
                    f(soft[:, r, 0, :], T[bank][:, :], ACT.Abs).then_inc(delta_act.sem, 1)
                    act.wait_ge(*delta_act.of(W, 3 * m + 1))
                    f(soft[:, r, 0, :], soft[:, r, 0, :], ACT.Exp, scale=-1.0).then_inc(delta_act.sem, 1)
                    act.wait_ge(*delta_act.of(W, 3 * m + 2))
                    f(soft[:, r, 1, :], soft[:, r, 0, :], ACT.Ln, bias=1.0).then_inc(delta_act.sem, 1)
                return step

            post = {"x1T": post_evacuate(0), "xnT": post_evacuate(1, g1, b1), "w_in": w_in_step, "conv1": conv1,
                    "xd": xd, "decay": decay_step, "y1": y1, "x3T": post_evacuate(2), "gate": gate,
                    "cwT": cw_transpose, **{f"expert{e}": expert(e) for e in range(E + 1)}}
            pre = {"x0T": x0T, "xz0": xz(0), "xz1": xz(1), "xz2": xz(2), "bc": bc, "bc_low": bc_low,
                   "delta0": delta_step(0), "delta1": delta_step(1), "delta2": delta_step(2)}

            def copy_rep(unit, g, i, s):
                n = 4 * g + 2 * i + s
                act.wait_ge(*rep_mm.of(unit, n + 1))
                if g >= 2 or unit.has_previous:
                    act.wait_ge(*weighted.of(unit, CI * (g - 1)))
                f(bc_rep[:, g % 2, i, s, :], rep[:, :], ACT.Copy).then_inc(rep_out.sem, 1)

            def decays(U, b):
                g, c = b // CI, b % CI
                if b == 0:
                    act.wait_ge(*delta_dve.of(U))
                if b >= NA or U.has_previous:
                    act.wait_ge(*scanned.of(U, b + 1 - NA))
                for s in range(NG):
                    n = NG * g + s
                    last = f(halves(decay[:, b % NA, s, :])[:, :, 1:], halves(delta[:, U.parity, c, :])[:, :, 1:],
                             ACT.Exp, scale=a_neg[:, c, n:n + 1])
                last.then_inc(decay_ready.sem, 1)

            def prologue(W):
                act.wait_ge(loaded, 5 * 16)
                al = w128[:, W128["a_log"][0]:W128["a_log"][0] + CI * DS]
                act.wait_ge(setup_dve, 3)
                f(al, al, ACT.Exp).then_inc(setup_act, 1)
                fw = w96[:, W96["ffn"][0]:W96["ffn"][0] + KM * DM]
                f(fw, fw, ACT.Sign).then_inc(setup_act, 1)
                act.wait_ge(setup_dve, SETUP_DVE)
                for s in sum(PRE, []):
                    if s in pre:
                        pre[s](W)
                for i in range(2):
                    for s in range(NG):
                        copy_rep(W, 0, i, s)

            def body(U, V, W):
                for b in range(BLOCKS):
                    decays(U, b)
                    for kind, s in PLAN[b]:
                        if kind == "post" and V and s in post:
                            post[s](V)
                        if kind == "pre" and W and s in pre:
                            pre[s](W)
                    unit, g = rep_target(U, W, b)
                    if unit:
                        for i, s in rep_jobs(b):
                            copy_rep(unit, g, i, s)

            def epilogue(V):
                for s in sum(POST, []):
                    if s in post:
                        post[s](V)

            run_units(act, prologue, body, epilogue)

        @block.vector
        def _(dve):
            v = nc.vector

            def norm_stats(unit, src, stat, before):
                for k in range(TILES):
                    v.bn_stats(stats[:, k, :], src[:, k, :]).then_inc(stat.sem, 1)
                dve.wait_ge(*stat.of(unit, before + TILES))
                v.memset(spare[:, :], 0.0)
                for k in range(TILES):
                    v.bn_aggr(mv[:, k, :], stats[:, k, :]).then_inc(stat.sem, 1)

            def norm_apply(unit, dst, src, rst, norm, n):
                dve.wait_ge(*rst.of(unit, 2 * n + 2))
                for k in range(TILES):
                    v.tensor_scalar(dst[:, k, :], src[:, k, :], mv[:, k, 0:1], rstd[:, k:k + 1], ALU.subtract,
                                    ALU.mult).then_inc(norm.sem, 1)

            def res1(V):
                if V.has_previous:
                    dve.wait_ge(*out_done.before(V))
                for b in range(2):
                    dve.wait_ge(*outproj_pe.of(V, b + 1))
                    v.scalar_tensor_tensor(xs[:, 2 * b:2 * b + 2, :], h0[:, V.parity, 2 * b:2 * b + 2, :], 2.0,
                                           two(b), ALU.mult, ALU.add).then_inc(res_dve.sem, 1)
                dve.wait_ge(*res_dve.of(V, 2))
                norm_stats(V, xs, post_stats, 0)

            def residual(n, pe_signal, bank, stat):
                def step(V):
                    for b in range(2):
                        dve.wait_ge(*pe_signal.of(V, b + 1 if pe_signal is not expert_down else None))
                        v.tensor_tensor(xs[:, 2 * b:2 * b + 2, :], xs[:, 2 * b:2 * b + 2, :], two(bank + b),
                                        ALU.add).then_inc(res_dve.sem, 1)
                    dve.wait_ge(*res_dve.of(V, 2 * n))
                    norm_stats(V, xs, post_stats, 8 * stat)
                return step

            def norm(n, dst):
                def step(V):
                    norm_apply(V, dst, xs, post_rstd, post_norm, n)
                    if n == 1:
                        dve.wait_ge(*post_norm.of(V, 2 * TILES))
                        norm_stats(V, xs, post_stats, 16)
                return step

            def conv1(V):
                for t in range(TAPS1):
                    for m in range(CI):
                        src = convin[:, m, :, PAD - TAPS1 + 1 + t:PAD - TAPS1 + 1 + t + L]
                        w = cw1[:, m, t:t + 1]
                        if t == 0:
                            dve.wait_ge(*w_in_act.of(V, m + 1))
                            v.tensor_scalar(halves(act1[:, m, :]), src, w, cb1[:, m:m + 1], ALU.mult,
                                            ALU.add).then_inc(conv1_dve.sem, 1)
                        else:
                            dve.wait_ge(*conv1_dve.of(V, CI * (t - 1) + m + 1))
                            v.scalar_tensor_tensor(halves(act1[:, m, :]), src, w, halves(act1[:, m, :]), ALU.mult,
                                                   ALU.add).then_inc(conv1_dve.sem, 1)

            def gate1(V):
                for m in range(CI):
                    dve.wait_ge(*conv1_act.of(V, m + 1))
                    v.scalar_tensor_tensor(act1[:, m, :], th[:, m, :], 1.0, act1[:, m, :], ALU.add,
                                           ALU.mult).then_inc(conv1_dve.sem, 1)

            def dt_step(V):
                dve.wait_ge(*xd_act.of(V))
                v.memset(halves(s_az)[:, :, 0:1], 0.0).then_inc(dt_dve.sem, 1)
                v.scalar_tensor_tensor(s_dt, s_e, 0.69, s_dt, ALU.mult, ALU.max).then_inc(dt_dve.sem, 1)
                dve.wait_ge(*dt_dve.of(V, 2))
                v.scalar_tensor_tensor(s_dt, s_x, 0.0, s_dt, ALU.max, ALU.add).then_inc(dt_dve.sem, 1)
                dve.wait_ge(*dt_dve.of(V, 3))
                v.tensor_tensor(halves(s_k), halves(s_dt), twice(ktab), ALU.mult).then_inc(dt_dve.sem, 1)

            def states_step(V):
                n = [0]

                def then(ins):
                    n[0] += 1
                    ins.then_inc(states_dve.sem, 1)
                    dve.wait_ge(*states_dve.of(V, n[0]))

                dve.wait_ge(*decay_act.of(V))
                then(v.tensor_tensor(s_ds, s_ds, s_e, ALU.mult))
                then(v.tensor_tensor_scan(s_v, s_az, s_ds, 0.0, ALU.mult, ALU.add))
                then(v.tensor_tensor(s_v, s_p, s_v, ALU.mult))
                then(v.scalar_tensor_tensor(s_k, s_p, 1.0, s_k, ALU.add, ALU.mult))
                then(v.scalar_tensor_tensor(s_x, s_x, 1.0, s_t, ALU.add, ALU.mult))
                then(v.tensor_scalar(s_x, s_x, 1e-30, None, ALU.max))
                then(v.reciprocal(s_x, s_x))
                then(v.tensor_tensor(s_k, s_k, s_x, ALU.mult))
                then(v.tensor_tensor(s_k, s_k, s_ds, ALU.mult))
                then(v.tensor_tensor(s_v, s_v, s_k, ALU.add))

            def route(V):
                n = [0]

                def then(ins):
                    n[0] += 1
                    ins.then_inc(route_dve.sem, 1)
                    dve.wait_ge(*route_dve.of(V, n[0]))

                def wide(ap, a, b, axis):
                    return ap.unsqueeze(axis).broadcast_to([128, TILES, a, b])

                G = E // 2
                dve.wait_ge(*gate_act.of(V))
                then(v.tensor_scalar(r_score, r_score, 0.5, 0.5, ALU.mult, ALU.add))
                s3 = r_s.rearrange("p (k e) -> p k e", e=E)
                then(v.tensor_tensor(s3, r_score.rearrange("p (k e) -> p k e", e=E),
                                     gbias.unsqueeze(1).broadcast_to([128, TILES, E]), ALU.add))
                then(v.tensor_tensor(r_g, r_s[:, 0::2], r_s[:, 1::2], ALU.add))
                then_rank(v, then, r_g.rearrange("p (k g) -> p k g", g=G), G, lt4, r_gsel, wide)
                then(v.tensor_scalar(r_off, r_gsel, BIG, -BIG, ALU.mult, ALU.add))
                pair = [128, TILES * G, 2]
                m3 = r_m.rearrange("p (g e) -> p g e", e=2)
                then(v.tensor_tensor(m3, r_s.rearrange("p (g e) -> p g e", e=2),
                                     r_gsel.unsqueeze(2).broadcast_to(pair), ALU.mult))
                then(v.tensor_tensor(m3, m3, r_off.unsqueeze(2).broadcast_to(pair), ALU.add))
                then_rank(v, then, r_m.rearrange("p (k e) -> p k e", e=E), E, lt8, r_sel, wide)
                then(v.tensor_tensor(r_cw, r_score, r_sel, ALU.mult))
                then(v.tensor_reduce(r_sum, r_cw.rearrange("p (k e) -> p k e", e=E), AX.X, ALU.add))
                then(v.tensor_scalar(r_sum, r_sum, 1e-6, None, ALU.add))
                then(v.reciprocal(r_sum, r_sum))
                c3 = r_cw.rearrange("p (k e) -> p k e", e=E)
                then(v.tensor_tensor(c3, c3, r_sum.unsqueeze(2).broadcast_to([128, TILES, E]), ALU.mult))
                h3 = hb[:, :].rearrange("p (k e) -> p k e", e=E)
                then(v.tensor_copy(h3, c3))
                then(v.tensor_copy(cws[:, :, 0:E], h3))
                then(v.tensor_tensor(c3, c3, h3, ALU.subtract))
                then(v.tensor_copy(h3, c3))
                then(v.tensor_copy(cws[:, :, E:2 * E], h3))
                then(v.tensor_tensor(cws[:, :, 2 * E:3 * E], c3, h3, ALU.subtract))
                assert n[0] == ROUTE_OPS

            def then_rank(v, then, val, n, lower, dst, wide):
                me, other = wide(val, n, n, 3), wide(val, n, n, 2)
                gt = r_gt[:, 0:TILES * n * n].rearrange("p (k a b) -> p k a b", a=n, b=n)
                eq = r_eq[:, 0:TILES * n * n].rearrange("p (k a b) -> p k a b", a=n, b=n)
                then(v.tensor_tensor(gt, other, me, ALU.is_gt))
                then(v.tensor_tensor(eq, other, me, ALU.is_equal))
                then(v.tensor_tensor(eq, eq, lower.unsqueeze(1).broadcast_to([128, TILES, n, n]), ALU.mult))
                then(v.tensor_tensor(gt, gt, eq, ALU.add))
                then(v.tensor_reduce(dst.rearrange("p (k a) -> p k a", a=n), gt, AX.X, ALU.add))
                then(v.tensor_scalar(dst, dst, 2.0, None, ALU.is_lt))

            def expert(e):
                def step(V):
                    dve.wait_ge(*expert_tanh.of(V, e + 1))
                    if e >= 2:
                        dve.wait_ge(*expert_down.of(V, e - 1))
                    v.scalar_tensor_tensor(hid[:, e % 2, :], th[:, e % 3, :], 1.0, T[0][:, :], ALU.add,
                                           ALU.mult).then_inc(expert_hid.sem, 1)
                    dve.wait_ge(*expert_up.of(V, 2 * e + 2))
                    dve.wait_ge(*expert_hid.of(V, 2 * e + 1))
                    v.tensor_tensor(hid[:, e % 2, :], hid[:, e % 2, :], T[1][:, :],
                                    ALU.mult).then_inc(expert_hid.sem, 1)
                return step

            def gather(W):
                for ch in range(CH):
                    dve.wait_ge(*gather_pe.of(W, ch + 1))
                    v.tensor_tensor(halves(masked[:, ch, :]), halves(T[ch][0:SIDE, :]), twice(col_hot[:, :]),
                                    ALU.mult).then_inc(gather_dve.sem, 1)

            def embed(W):
                for b in range(2):
                    dve.wait_ge(*embed_pe.of(W, b + 1))
                    v.tensor_tensor(h0[:, W.parity, 2 * b:2 * b + 2, :], two((3, 0)[b]),
                                    pb.unsqueeze(1).broadcast_to([128, 2, DM]), ALU.add).then_inc(embed_dve.sem, 1)
                dve.wait_ge(*embed_dve.of(W))
                norm_stats(W, h0[:, W.parity], pre_stats, 0)

            def norm0(W):
                norm_apply(W, xn, h0[:, W.parity], pre_rstd, pre_norm, 0)

            def xc_gate(W, m):
                dve.wait_ge(*xz_act.of(W, 3 * m + 3))
                v.scalar_tensor_tensor(xc[:, m, :], th[:, 1, :], 1.0, xc[:, m, :], ALU.add,
                                       ALU.mult).then_inc(xz_dve.sem, 1)

            def xz(m):
                def step(W):
                    if m:
                        xc_gate(W, m - 1)
                    elif W.has_previous:
                        dve.wait_ge(*diag_in.before(W))
                        dve.wait_ge(*delta_pool.before(W))
                    n = 9 * m
                    dve.wait_ge(*xz_act.of(W, 3 * m + 1))
                    for t in range(TAPS0):
                        src, w = convin[:, m, :, t:t + L], cw0[:, m, t:t + 1]
                        if t == 0:
                            v.tensor_scalar(halves(xc[:, m, :]), src, w, cb0[:, m:m + 1], ALU.mult,
                                            ALU.add).then_inc(xz_dve.sem, 1)
                        else:
                            dve.wait_ge(*xz_dve.of(W, n + t))
                            v.scalar_tensor_tensor(halves(xc[:, m, :]), src, w, halves(xc[:, m, :]), ALU.mult,
                                                   ALU.add).then_inc(xz_dve.sem, 1)
                    dve.wait_ge(*xz_act.of(W, 3 * m + 2))
                    v.scalar_tensor_tensor(gz[:, W.parity, m, :], th[:, 0, :], 1.0, T[1][:, :], ALU.add,
                                           ALU.mult).then_inc(xz_dve.sem, 1)
                return step

            def xc_end(W):
                xc_gate(W, CI - 1)

            def bc(W):
                for i in range(2):
                    dve.wait_ge(*bc_act.of(W, i + 1))
                    v.scalar_tensor_tensor(low[:, i, :], hi16[:, i, :], m1, T[i][0:96, :], ALU.mult,
                                           ALU.add).then_inc(bc_dve.sem, 1)

            def bc_low(W):
                for i in range(2):
                    dve.wait_ge(*bc_act.of(W, i + 3))
                    v.scalar_tensor_tensor(bc_st[:, W.parity, i, :], hi16[:, i, :], m2, low[:, i, :], ALU.mult,
                                           ALU.add).then_inc(bc_dve.sem, 1)

            def delta_step(m):
                def step(W):
                    bank, r = (2, 3, 0)[m], m % 2
                    dve.wait_ge(*delta_act.of(W, 3 * m + 3))
                    v.scalar_tensor_tensor(soft[:, r, 1, :], soft[:, r, 0, :], 0.69, soft[:, r, 1, :], ALU.mult,
                                           ALU.max).then_inc(delta_dve.sem, 1)
                    dve.wait_ge(*delta_dve.of(W, 2 * m + 1))
                    v.scalar_tensor_tensor(delta[:, W.parity, m, :], T[bank][:, :], 0.0, soft[:, r, 1, :], ALU.max,
                                           ALU.add).then_inc(delta_dve.sem, 1)
                return step

            post = {"res1": res1, "norm1": norm(0, xs), "res2": residual(2, ffn_pe, 0, 1), "norm2": norm(1, xs),
                    "prenorm": norm(2, xn), "conv1": conv1, "gate1": gate1, "dt": dt_step, "states": states_step,
                    "res3": residual(3, w_out_pe, 2, 3), "norm3": norm(3, xs), "route": route,
                    "experts_end": residual(4, expert_down, 2, 4), "norm4": norm(4, xs),
                    **{f"expert{e}": expert(e) for e in range(E + 1)}}
            pre = {"gather": gather, "embed": embed, "norm0": norm0, "xz0": xz(0), "xz1": xz(1), "xz2": xz(2),
                   "xc_end": xc_end, "bc": bc, "bc_low": bc_low,
                   "delta0": delta_step(0), "delta1": delta_step(1), "delta2": delta_step(2)}

            def scan(U, b):
                g, c = b // CI, b % CI
                mine, pools = drives(b)
                if on_pool(b):
                    dve.wait_ge(*drive_pool.of(U, pools))
                else:
                    dve.wait_ge(*rep_out.of(U, 4 * g + 2))
                    if b < CI:
                        dve.wait_ge(*delta_pool.of(U))
                    if b >= NX or U.has_previous:
                        dve.wait_ge(*summed.of(U, b + 1 - NX))
                    v.tensor_tensor(drive[:, b % NX], du[:, U.parity, c, :].unsqueeze(1).broadcast_to([128, NG, TOK]),
                                    bc_rep[:, g % 2, 0], ALU.mult).then_inc(drive_dve.sem, 1)
                    dve.wait_ge(*drive_dve.of(U, mine))
                dve.wait_ge(*decay_ready.of(U, b + 1))
                flat = drive[:, b % NX].rearrange("p s t -> p (s t)")
                v.tensor_tensor_scan(flat, decay[:, b % NA].rearrange("p s t -> p (s t)"), flat, 0.0, ALU.mult,
                                     ALU.add).then_inc(scanned.sem, 1)

            def tail(V):
                for c in range(CI):
                    dve.wait_ge(*summed.of(V, BLOCKS - CI + c + 1))
                    v.tensor_tensor(act1[:, c, :], y[c][:, :], gz[:, V.parity, c, :],
                                    ALU.mult).then_inc(gated.sem, 1)

            def prologue(W):
                n = [0]

                def setup(ins):
                    n[0] += 1
                    ins.then_inc(setup_dve, 1)

                setup(v.memset(decay[:, :, :, :], 0.0))
                setup(v.memset(convin[:, :, :, :], 0.0))
                dve.wait_ge(loaded, 5 * 16)
                al = w128[:, W128["a_log"][0]:W128["a_log"][0] + CI * DS]
                setup(v.tensor_scalar(al, al, LOG_MAX, None, ALU.min))
                setup(v.tensor_scalar(row_hot[:, :], curve_i[:, 1, :], part, None, ALU.is_equal))
                setup(v.tensor_scalar(col_hot[:, :], curve_i[:, 0, :], part, None, ALU.is_equal))
                for name, w in (("cw0", CI * TAPS0), ("cb0", CI), ("cw1", CI * TAPS1), ("cb1", CI)):
                    ap = w128[:, W128[name][0]:W128[name][0] + w]
                    setup(v.tensor_scalar(ap, ap, 0.5, None, ALU.mult))
                setup(v.tensor_scalar(win[:, :, DI:], win[:, :, DI:], 0.5, None, ALU.mult))
                setup(v.tensor_scalar(w1, w1, 0.5, None, ALU.mult))
                setup(v.tensor_tensor(by1, by1, by2, ALU.add))
                for c in range(CI):
                    setup(v.tensor_scalar(diag_d[:, c, :], ident, dskip[:, c:c + 1], None, ALU.mult))
                dve.wait_ge(setup_act, 1)
                setup(v.tensor_scalar(al, al, -1.0, None, ALU.mult))
                assert n[0] == SETUP_DVE
                dve.wait_ge(setup_dve, SETUP_DVE)
                for s in sum(PRE, []):
                    if s in pre:
                        pre[s](W)

            def body(U, V, W):
                for b in range(BLOCKS):
                    scan(U, b)
                    if b == TAIL_BLOCK and V:
                        tail(V)
                    for kind, s in PLAN[b]:
                        if kind == "post" and V and s in post:
                            post[s](V)
                        if kind == "pre" and W and s in pre:
                            pre[s](W)

            def epilogue(V):
                tail(V)
                for s in sum(POST, []):
                    if s in post:
                        post[s](V)

            run_units(dve, prologue, body, epilogue)

        @block.gpsimd
        def _(pool):
            g_ = nc.gpsimd

            def rstd_step(n, stat, rst):
                def step(unit):
                    pool.wait_ge(*stat.of(unit, 8 * (n + 1)))
                    g_.tensor_tensor(rstd[:, :], mv[:, :, 1], eps, ALU.add).then_inc(rst.sem, 1)
                    pool.wait_ge(*rst.of(unit, 2 * n + 1))
                    g_.tensor_tensor(rstd[:, :], rstd[:, :], half, ALU.pow).then_inc(rst.sem, 1)
                return step

            def expert(e):
                def step(V):
                    pool.wait_ge(*expert_hid.of(V, 2 * e + 2))
                    pool.wait_ge(*crep_out.of(V, e + 1))
                    g_.tensor_tensor(hid[:, e % 2, :], hid[:, e % 2, :], crep[:, e % 2, :],
                                     ALU.mult).then_inc(expert_scaled.sem, 1)
                return step

            def delta_step(m):
                def step(W):
                    pool.wait_ge(*delta_dve.of(W, 2 * m + 2))
                    g_.tensor_tensor(du[:, W.parity, m, :], delta[:, W.parity, m, :], xc[:, m, :],
                                     ALU.mult).then_inc(delta_pool.sem, 1)
                return step

            post = {"res1": rstd_step(0, post_stats, post_rstd), "res2": rstd_step(1, post_stats, post_rstd),
                    "norm2": rstd_step(2, post_stats, post_rstd), "res3": rstd_step(3, post_stats, post_rstd),
                    "experts_end": rstd_step(4, post_stats, post_rstd), **{f"expert{e}": expert(e) for e in range(E)}}
            pre = {"embed": rstd_step(0, pre_stats, pre_rstd), "delta0": delta_step(0), "delta1": delta_step(1),
                   "delta2": delta_step(2)}

            def drive_block(U, b):
                g, c = b // CI, b % CI
                pool.wait_ge(*rep_out.of(U, 4 * g + 2))
                if b < CI:
                    pool.wait_ge(*delta_pool.of(U))
                if b >= NX or U.has_previous:
                    pool.wait_ge(*summed.of(U, b + 1 - NX))
                g_.tensor_tensor(drive[:, b % NX], du[:, U.parity, c, :].unsqueeze(1).broadcast_to([128, NG, TOK]),
                                 bc_rep[:, g % 2, 0], ALU.mult).then_inc(drive_pool.sem, 1)

            def weigh(U, b):
                pool.wait_ge(*scanned.of(U, b + 1))
                pool.wait_ge(*rep_out.of(U, 4 * (b // CI) + 4))
                g_.tensor_tensor(drive[:, b % NX], drive[:, b % NX], bc_rep[:, (b // CI) % 2, 1],
                                 ALU.mult).then_inc(weighted.sem, 1)

            def prologue(W):
                pool.wait_ge(setup_dve, SETUP_DVE)
                for s in sum(PRE, []):
                    if s in pre:
                        pre[s](W)

            def body(U, V, W):
                for b in range(BLOCKS):
                    if b + 1 < BLOCKS and on_pool(b + 1):
                        drive_block(U, b + 1)
                    weigh(U, b)
                    for kind, s in PLAN[b]:
                        if kind == "post" and V and s in post:
                            post[s](V)
                        if kind == "pre" and W and s in pre:
                            pre[s](W)

            def epilogue(V):
                for s in sum(POST, []):
                    if s in post:
                        post[s](V)

            run_units(pool, prologue, body, epilogue)


def pack(parts, layout, width, rows):
    packed = np.zeros((rows, width), np.float32)
    for name, a in parts.items():
        start, w = layout[name]
        a = a.reshape(a.shape[0], -1)
        assert a.shape[1] == w, (name, a.shape, w)
        packed[:a.shape[0], start:start + w] = a
    return packed


def chunks(w, rows):
    return w.reshape(w.shape[0] // rows, rows, -1).transpose(1, 0, 2)


def per_channel(a, rows):
    return a.reshape(a.shape[0] // rows, rows, -1).transpose(1, 0, 2)


def layout(i):
    wx = i["L0_attn_Wx"].T
    bc = np.concatenate([wx[:, 0:DS]] * 3 + [wx[:, DS:2 * DS]] * 3, axis=1)
    wo = i["L1_attn_W_out"]
    wo_x = np.zeros((256, DM), np.float32)
    wo_x[64:128] = wo[DM:256]
    wo_x[128:256] = wo[256:384]
    wsd = np.zeros((DI, 48), np.float32)
    wsd[:, 0:N16] = i["L1_attn_W_dt"]
    wsd[:, 32:48] = i["L1_attn_W_xp"][:, DM:]
    up = lambda w, s: np.concatenate([w, s[None]], 0).transpose(2, 0, 1).reshape(DM, -1)
    w2 = np.concatenate([i["L1_ffn_w2"], i["L1_ffn_sw2"][None]], 0).transpose(2, 0, 1)
    third = np.arange(96) // DS
    b_ds = np.zeros((48, 1), np.float32)
    b_ds[32:48, 0] = i["L1_attn_b_xp"][DM:]
    earlier = lambda n: np.tril(np.ones((n, n), np.float32), -1)
    rows = lambda a, n: np.broadcast_to(np.asarray(a, np.float32).reshape(1, -1), (n, np.asarray(a).size))
    p128 = pack({
        "ident": np.eye(128), "wx_bc": chunks(bc, 128), "wx_d": chunks(wx[:, 2 * DS:], 128),
        "wout": chunks(i["L0_attn_Wout"].T, 128), "wo_x": chunks(wo_x, 128),
        "wxp": chunks(i["L1_attn_W_xp"][:, 0:DM], 128), "wsd": chunks(wsd, 128), "w2": w2,
        "a_log": per_channel(i["L0_attn_A_log"], 128), "cw0": per_channel(i["L0_attn_conv_w"][:, 0], 128),
        "cb0": per_channel(i["L0_attn_conv_b"], 128), "dskip": per_channel(i["L0_attn_D"], 128),
        "b_in": per_channel(i["L1_attn_b_in"], 128), "cw1": per_channel(i["L1_attn_W_conv"][:, 0], 128),
        "cb1": per_channel(i["L1_attn_b_conv"], 128), "part": np.arange(128)[:, None],
        "m1": np.where(third >= 1, -1, 0)[:, None], "m2": np.where(third >= 2, -1, 0)[:, None],
        "pw": rows(i["L0_tok_proj_w"].T, SIDE), "pb": rows(i["L0_tok_proj_b"], 128),
        "gbias": rows(i["L1_ffn_gate_bias"], 128), "ones": np.ones((1, 128)), "b_out": i["L1_attn_b_out"][None],
        "b_dt": i["L1_attn_b_dt"][:, None], "b_ds": b_ds, "k": rows(np.arange(L - 1, -1, -1), N16),
        "w_us": i["L1_attn_W_us"], "lt4": rows(earlier(4), 128), "lt8": rows(earlier(8), 128),
        "half": np.full((128, TILES), -0.5), "eps": np.full((128, TILES), EPS)}, W128, N128, 128)
    p96 = pack({
        "win": chunks(i["L0_attn_Win"].T, KC), "ffn": chunks(i["L0_ffn_weight"].T, KC),
        "w_in": chunks(i["L1_attn_W_in"], KC), "wo_y": chunks(wo[0:DM], KC),
        "gate": chunks(i["L1_ffn_gate_weight"].T, KC), "w1": chunks(up(i["L1_ffn_w1"], i["L1_ffn_sw1"]), KC),
        "w3": chunks(up(i["L1_ffn_w3"], i["L1_ffn_sw3"]), KC), "g0": per_channel(i["L0_attn_ln_g"], KC),
        "b0": per_channel(i["L0_attn_ln_b"], KC), "g1": per_channel(i["L1_attn_ln_g"], KC),
        "b1": per_channel(i["L1_attn_ln_b"], KC), "by1": per_channel(i["L1_attn_b_xp"][0:DM], KC),
        "by2": per_channel(i["L1_attn_b_us"], KC)}, W96, N96, KC)
    bf = _mybir_np(BF16)
    one_of = lambda n: np.repeat(np.tile(np.eye(n, dtype=np.float32), (3, 1)), 128, axis=1).astype(bf)
    return {"x": i["x"].reshape(IMAGES * CH, SIDE, SIDE), "curve": np.ascontiguousarray(i["L0_tok_curve"].T),
            "p128": p128, "p96": p96, "sel": one_of(DS), "sel_e": one_of(E)}


def _mybir_np(dt):
    return mybir.dt.np(dt)


def declare(nc, arrays, units=UNITS):
    aps = [nc.dram_tensor(f"in_{n}", a.shape, mybir.dt.from_np(a.dtype), kind="ExternalInput").ap()
           for n, a in arrays.items()]
    out = nc.dram_tensor("result", (IMAGES * L, DM), F32, kind="ExternalOutput").ap()
    build(nc, *aps, out, units=units)


def kernel(**inputs):
    import concourse.bacc as bacc
    from concourse.bass_utils import run_bass_kernel_spmd

    arrays = layout({k: np.asarray(a) for k, a in inputs.items()})
    nc = bacc.Bacc("TRN2", target_bir_lowering=False, num_devices=1)
    declare(nc, arrays)
    got = run_bass_kernel_spmd(nc, [{f"in_{n}": a for n, a in arrays.items()}], core_ids=[0])
    return got.results[0]["result"].reshape(IMAGES, L, DM)
```

```python
import concourse.bass as bass
from concourse import mybir
from contextlib import ExitStack
import numpy as np

F32, BF16, I32 = mybir.dt.float32, mybir.dt.bfloat16, mybir.dt.int32
ALU, ACT, AX = mybir.AluOpType, mybir.ActivationFunctionType, mybir.AxisListType

IMAGES, CH, SIDE = 64, 3, 112
L, DM, DI, DS = 256, 192, 384, 32
TAPS0, TAPS1, N16 = 7, 4, 16
TAPS_A = 3
E, INTER = 8, 128
PAIR = 2
TOK = PAIR * L
UNITS = IMAGES // PAIR
TILES = TOK // 128
KC, KM = 96, DM // 96
CI = DI // 128
NG = 2
GROUPS = DS // NG
BLOCKS = GROUPS * CI
NA, NX = 2, 4
REP_FRONT, REP_BEHIND = ((0,), (1,), (3,)), ((), (2,), ())
LAG = 2
ROUTE_OPS, SETUP_DVE, SETUP_ACT = 29, 20, 2
LOG_MAX = 88.0
PAD = TAPS0 - 1
EPS = 1e-5
BIG = 3.0e38


def columns(widths):
    at, start = {}, 0
    for name, w in widths:
        at[name] = (start, w)
        start += w
    return at, start


W128, N128 = columns([
    ("ident", 128), ("wx_bc", CI * 192), ("wx_d", CI * DI), ("wout", CI * DM), ("w_y", CI * DM),
    ("wdd", CI * 64), ("w2", (E + 1) * DM), ("a_log", CI * DS), ("cw0", CI * TAPS0),
    ("cb0", CI), ("dskip", CI), ("b_in", CI), ("cw1", CI * TAPS1), ("cb1", CI), ("part", 1), ("m1", 1),
    ("m2", 1), ("pw", CH * DM), ("pb", DM), ("gbias", E), ("b_out", DM), ("b_dt", 1),
    ("b_ds", 1), ("k", L), ("lt4", 16), ("lt8", 64), ("half", TILES), ("eps", TILES)])
W96, N96 = columns([
    ("win", KM * 2 * DI), ("ffn", KM * DM), ("w_in", KM * DI), ("gate", KM * E),
    ("w1", KM * (E + 1) * INTER), ("w3", KM * (E + 1) * INTER), ("g0", KM), ("b0", KM), ("g1", KM),
    ("b1", KM)])
FOLD, NFOLD = columns([("wxpT", KM * DI), ("w_usT", KM * PAIR * 32), ("by1", KM * 128), ("by2", KM * 128), ("wo_y", KM * DM)])

POST = [["outproj", "res1"], ["norm1"], ["x1T"], ["ffn", "res2"], ["norm2"], ["prenorm"], ["xnT"],
        ["conv1_0"], ["conv1_1"], ["conv1_2"], ["gate1"], ["xd"], ["dt"], ["decay", "states"],
        ["w_out", "res3"], ["norm3"], ["x3T"], ["gate", "route0"], ["route1"], ["route2"], ["cwT"]]
EXPERTS = sum([[[f"expert{e}"], [f"down{e}"]] for e in range(E + 1)], []) + [["res4"], ["norm4"]]
PRE = [["gather"], ["embed"], ["norm0"], ["x0T"], ["xz0"], ["conv0_0"], ["xz1"], ["conv0_1"], ["xz2"], ["conv0_2"],
       ["xc_end"], ["bc"], ["bc_low"], ["delta0"], ["delta1"], ["delta2"], ["soft"]]
POST_AT = (2, 3, 6, 9, 10, 14, 17, 21, 23, 25, 26, 29, 31, 32, 36, 37, 38, 39, 40, 42, 44)
PRE_AT = (1, 3, 5, 8, 11, 12, 14, 16, 18, 27, 30, 32, 35, 37, 40, 42, 43)
EXPERTS_AT = (45, 47, 48, 52, 53, 55, 57, 58, 60, 63, 64, 68, 70, 73, 74, 78, 79, 81, 82, 83)
PLAN = {b: [] for b in range(BLOCKS)}


def place(rows, blocks, plan, kind):
    assert len(rows) == len(blocks) and list(blocks) == sorted(blocks)
    for row, b in zip(rows, blocks):
        plan[b % BLOCKS] += [(kind(b), s) for s in row]


def fill(plan):
    place(EXPERTS, EXPERTS_AT, plan, lambda b: "late" if b < BLOCKS else "early")
    place(POST, POST_AT, plan, lambda b: "post")
    place(PRE, PRE_AT, plan, lambda b: "pre")


fill(PLAN)
TAIL_AT = (0, 1, 2)
POOL_DRIVES = (1, 4, 7, 10, 13, 16, 19, 22, 25, 28, 31, 34, 37, 39, 43, 46)


class Unit:

    def __init__(self, n, parity):
        self.n, self.parity = n, parity
        self.has_previous = not isinstance(n, int) or n > 0

    def nth(self, per_unit, k):
        return self.n * per_unit + k

    def before(self, per_unit, k):
        return self.n * per_unit + (k - per_unit)


def build(nc, x, curve, p128, p96, fold, sel, sel_e, out, units=UNITS):
    ctx = ExitStack()
    with ctx:
        def sb(name, shape, dt=F32):
            return ctx.enter_context(nc.sbuf_tensor(name, shape, dt))

        def sem(name):
            return ctx.enter_context(nc.semaphore(name))

        w128, w96 = sb("w128", [128, N128]), sb("w96", [KC, N96])
        sel_sb = sb("sel_sb", [96 + 3 * E, DS, 128], BF16)
        sel_e_sb = sel_sb[96:, 0:E, :]
        row_hot, col_hot = sb("row_hot", [SIDE, L]), sb("col_hot", [SIDE, L])
        diag_d = sb("diag_d", [128, CI, 128])

        def p(name, rows=128, **dims):
            a, w = W128[name]
            v = w128[0:rows, a:a + w]
            return v.rearrange("p (a b) -> p a b", **dims) if dims else v

        def q(name, **dims):
            a, w = W96[name]
            v = w96[:, a:a + w]
            return v.rearrange("p (a b) -> p a b", **dims) if dims else v

        ident = p("ident")
        wx_bc, wx_d, wout = p("wx_bc", a=CI), p("wx_d", a=CI), p("wout", a=CI)
        w_y, w2 = p("w_y", a=CI), p("w2", a=E + 1)
        wdd = p("wdd", a=CI)
        a_neg, cw0, cb0, dskip = p("a_log", a=CI), p("cw0", a=CI), p("cb0"), p("dskip")
        b_in, cw1, cb1, part = p("b_in"), p("cw1", a=CI), p("cb1"), p("part", SIDE)
        m1, m2, pw, pb = p("m1", 96), p("m2", 96), p("pw", SIDE, a=CH), p("pb")
        gbias, b_out, b_dt, b_ds = p("gbias"), p("b_out"), p("b_dt", 2 * 32), p("b_ds", 2 * 32)
        ktab, lt4, lt8, half, eps = p("k", 2 * 32), p("lt4", a=4), p("lt8", a=8), p("half"), p("eps")
        win, ffn_w, w_in = q("win", a=KM), q("ffn", a=KM), q("w_in", a=KM)
        gate_w, w1, w3 = q("gate", a=KM), q("w1", a=KM), q("w3", a=KM)
        g0, b0, g1, b1 = (q(n) for n in ("g0", "b0", "g1", "b1"))
        w_us = sb("w_us", [PAIR * 32, DM])

        decay = sb("decay", [128, NA, NG, TOK])
        drive = sb("drive", [128, NX, NG, TOK])
        fold_sb = drive[:, :, :, :].rearrange("p a b c -> p (a b c)")[0:KC, 0:NFOLD]
        wxpT, w_usT, by1, by2, wo_y = (
            fold_sb[:, FOLD[n][0]:FOLD[n][0] + FOLD[n][1]].rearrange("p (a b) -> p a b", a=KM)
            for n in ("wxpT", "w_usT", "by1", "by2", "wo_y"))
        bc_rep = sb("bc_rep", [128, 2, 2, NG, TOK])
        delta, du, gz = (sb(n, [128, 2, CI, TOK]) for n in ("delta", "du", "gz"))
        stacks = sb("stacks", [96 + 3 * E, 2, 2, TOK], BF16)
        bc_st = stacks[0:96]
        cwT = stacks[96:, 0, 0, :]
        xc = sb("xc", [128, CI, TOK])
        h0 = sb("h0", [128, 2, TILES, DM])
        xs = sb("xs", [128, TILES, DM])
        xT = sb("xT", [KC, KM, TOK])
        act1 = sb("act1", [128, CI, TOK])
        xn1 = act1[:, :, :].rearrange("p c t -> p (c t)")[:, 0:TILES * DM].rearrange("p (k d) -> p k d", k=TILES)
        th = sb("th", [128, 2, TOK])
        th1 = th[:, 1, :]
        stats, mv, rstd = sb("stats", [128, TILES, 6]), sb("mv", [128, TILES, 2]), sb("rstd", [128, TILES])
        small = sb("small", [128, 7, L])
        convin1 = small[:, :, :].rearrange("p i t -> p (i t)")[:, 0:CI * PAIR * (TAPS1 - 1 + L)].rearrange(
            "p (c b t) -> p c b t", c=CI, b=PAIR)
        gt_ = act1[:, 0, 0:308]
        hb = sb("hb", [128, TILES * E], BF16)
        spare = sb("spare", [128, 2])
        convin0 = sb("convin0", [128, PAIR, PAD + L])
        stats0, mv0, rstd0 = sb("stats0", [128, TILES, 6]), sb("mv0", [128, TILES, 2]), sb("rstd0", [128, TILES])
        S = sb("S", [128, 5, TOK])
        curve_i = S[0:SIDE, 0, :].bitcast(I32).rearrange("p (a n) -> p a n", a=2)
        img = S[0:SIDE, 3:5, :].rearrange("p a t -> p (a t)")[:, 0:PAIR * CH * SIDE].rearrange(
            "p (c w) -> p c w", w=SIDE)
        masked = S[0:SIDE, 0:3, :]
        thz, thc = S[:, 3, :], S[:, 4, :]
        xn0 = S[:, 0:2, :].rearrange("p a t -> p (a t)")[:, 0:TILES * DM].rearrange("p (k d) -> p k d", k=TILES)
        x0T = S[0:KC, 1:3, :]
        low, hi16 = S[0:96, 0:2, :], S[0:96, 2, :].bitcast(BF16).rearrange("p (a t) -> p a t", a=2)
        soft_e = S[:, 2:5, :]
        xe = sb("xe", [128, TILES, DM])
        xeT = sb("xeT", [KC, KM, TOK])
        hid, crep = th[:, 0, :], sb("crep", [128, TOK])
        stats4, mv4, rstd4 = sb("stats4", [128, TILES, 6]), sb("mv4", [128, TILES, 2]), sb("rstd4", [128, TILES])
        s_x, s_e, s_dt, s_ds, s_k, s_p, s_v = (small[0:64, i, :] for i in range(7))
        s_t = th[0:64, 1, 0:L]
        r_score, r_s, r_m, r_sel, r_cw = (gt_[:, TILES * E * i:TILES * E * (i + 1)] for i in range(5))
        r_g, r_gsel, r_off = (gt_[:, 160 + 16 * i:176 + 16 * i] for i in range(3))
        r_sum, cws = gt_[:, 208:212], gt_[:, 212:308].rearrange("p (k e) -> p k e", e=3 * E)
        r_gt, r_eq = small[:, 0, 0:TILES * E * E], small[:, 1, 0:TILES * E * E]

        y = [ctx.enter_context(nc.psum_tensor(f"y{c}", [128, TOK], F32)) for c in range(CI)]
        rep = ctx.enter_context(nc.psum_tensor("rep", [128, TOK], F32))
        T = [ctx.enter_context(nc.psum_tensor(f"T{c}", [128, TOK], F32)) for c in range(4)]

        def two(bank):
            return T[bank][:, 0:2 * DM].rearrange("p (a d) -> p a d", a=2)

        def on_pool(b):
            return b in POOL_DRIVES

        def drives(b):
            pool = sum(on_pool(i) for i in range(b + 1))
            return b + 1 - pool, pool

        class Signal:
            def __init__(self, name, per_unit, step=1):
                self.sem, self.per_unit, self.step = sem(name), per_unit * step, step

            def of(self, unit, k=None):
                return self.sem, unit.nth(self.per_unit, self.per_unit if k is None else k * self.step)

            def before(self, unit, k=None):
                return self.sem, unit.nth(self.per_unit, 0 if k is None else k * self.step - self.per_unit)

        loaded, setup_act, setup_dve, setup_pe = (sem(n) for n in ("loaded", "setup_act", "setup_dve", "setup_pe"))
        img_in = Signal("img_in", 1, 16)
        out_done = Signal("out_done", 1, 16)
        rep_mm = Signal("rep_mm", 4 * GROUPS)
        rep_out = Signal("rep_out", 4 * GROUPS)
        decay_ready = Signal("decay_ready", BLOCKS)
        drive_dve = Signal("drive_dve", drives(BLOCKS - 1)[0])
        drive_pool = Signal("drive_pool", drives(BLOCKS - 1)[1])
        scanned = Signal("scanned", BLOCKS)
        weighted = Signal("weighted", BLOCKS)
        summed = Signal("summed", BLOCKS)
        diag_in = Signal("diag_in", CI)
        gated = Signal("gated", CI)
        post_stats = Signal("post_stats", 4 * 2 * TILES)
        post_rstd = Signal("post_rstd", 4 * 2)
        post_norm = Signal("post_norm", 4 * TILES)
        end_stats, end_rstd, end_norm = Signal("end_stats", 2 * TILES), Signal("end_rstd", 2), Signal("end_norm", TILES)
        pre_stats, pre_rstd, pre_norm = Signal("pre_stats", 2 * TILES), Signal("pre_rstd", 2), Signal("pre_norm", TILES)
        post_tp, post_xT = Signal("post_tp", 3 * KM), Signal("post_xT", 3 * KM)
        pre_tp, pre_xT = Signal("pre_tp", KM), Signal("pre_xT", KM)
        outproj_pe, ffn_pe, w_out_pe = Signal("outproj_pe", 2), Signal("ffn_pe", 2), Signal("w_out_pe", 2)
        res_dve, res4_dve = Signal("res_dve", 3 * 2), Signal("res4_dve", 2)
        w_in_pe, w_in_act = Signal("w_in_pe", CI), Signal("w_in_act", CI)
        pad_dve = Signal("pad_dve", 1)
        conv1_dve, conv1_act = Signal("conv1_dve", CI * TAPS1), Signal("conv1_act", CI)
        act1_dve = Signal("act1_dve", CI)
        xd_pe, xd_act, dt_dve = Signal("xd_pe", 1), Signal("xd_act", 8), Signal("dt_dve", 3)
        decay_act, states_dve = Signal("decay_act", 5), Signal("states_dve", 10)
        bias_pool = Signal("bias_pool", 1)
        gate_pe, gate_act, route_dve = Signal("gate_pe", 1), Signal("gate_act", 1), Signal("route_dve", ROUTE_OPS)
        cwT_pe, cwT_act = Signal("cwT_pe", 1), Signal("cwT_act", 1)
        expert_up = Signal("expert_up", 2 * (E + 1))
        expert_tanh = Signal("expert_tanh", E + 1)
        expert_hid = Signal("expert_hid", 2 * (E + 1))
        crep_mm, crep_out = Signal("crep_mm", E), Signal("crep_out", E)
        expert_scaled = Signal("expert_scaled", E)
        expert_down = Signal("expert_down", E + 1)
        gather_pe, gather_dve = Signal("gather_pe", CH), Signal("gather_dve", CH)
        embed_pe, embed_dve = Signal("embed_pe", 2), Signal("embed_dve", 2)
        xz_pe = Signal("xz_pe", 2 * CI)
        convin0_act, thz_act = Signal("convin0_act", CI), Signal("thz_act", CI)
        conv0_dve, conv0_act = Signal("conv0_dve", CI * TAPS0), Signal("conv0_act", CI)
        gz_dve, xc_dve = Signal("gz_dve", CI), Signal("xc_dve", CI)
        bc_pe, bc_act, bc_dve = Signal("bc_pe", 2), Signal("bc_act", 4), Signal("bc_dve", 4)
        delta_pe, abs_act, exp_act = Signal("delta_pe", CI), Signal("abs_act", CI), Signal("exp_act", CI)
        relu_act, ln_act = Signal("relu_act", CI), Signal("ln_act", 1)
        delta_dve, delta_pool = Signal("delta_dve", 2), Signal("delta_pool", CI)

        block = ctx.enter_context(nc.Block())

        def run_units(eng, prologue, body, epilogue):
            prologue(Unit(0, 0))

            def unit(n, parity, behind):
                there = not isinstance(n, int) or (n >= behind and n - behind < units)
                return Unit(n - behind, (parity + behind) % 2) if there else None

            def one(n, parity):
                body(*(unit(n, parity, behind) for behind in (0, 1, -1, 2)))

            one(0, 0)
            one(1, 1)
            if units > 4:
                with eng.Fori(1, units // 2 - 1) as j:
                    one(j * 2, 0)
                    one(j * 2 + 1, 1)
            if units > 2:
                one(units - 2, 0)
                one(units - 1, 1)
            epilogue(Unit(units - 1, 1), Unit(units - 2, 0))

        def sides(steps, V, W, X, only=None):
            of = {"post": V, "late": V, "pre": W, "early": X}
            return [(s, of[kind]) for kind, s in steps if of[kind] and (only is None or kind in only)]

        def rest(V, X):
            every = sum((PLAN[b] for b in range(BLOCKS)), [])
            return sides(every, V, None, X) + sides(every, None, None, V)

        def halves(ap):
            return ap.rearrange("p (b t) -> p b t", b=PAIR)

        def twice(ap):
            return ap.unsqueeze(1).broadcast_to([ap.shape[0], PAIR, L])

        def rep_jobs(b, when):
            jobs = {"front": REP_FRONT, "behind": REP_BEHIND}[when][b % CI]
            return [(i // NG, i % NG) for i in jobs]

        def rep_target(U, W, b):
            g = b // CI + 1
            return (U, g) if g < GROUPS else (W, 0)

        @block.sync
        def _(sp):
            sp.dma_start(w128[:, :], p128).then_inc(loaded, 16)
            sp.dma_start(w96[:, :], p96).then_inc(loaded, 16)
            sp.dma_start(fold_sb, fold).then_inc(loaded, 16)
            sp.dma_start(sel_sb[0:96, :, :], sel.rearrange("p (n m) -> p n m", n=DS)).then_inc(loaded, 16)
            sp.dma_start(sel_e_sb, sel_e.rearrange("p (n m) -> p n m", n=E)).then_inc(loaded, 16)
            sp.dma_start(curve_i[:, :, :],
                         curve.rearrange("(a c) n -> a c n", a=1).broadcast_to([SIDE, 2, L])).then_inc(loaded, 16)

            def load_images(W):
                if W.has_previous:
                    sp.wait_ge(*delta_dve.before(W, 1))
                sp.dma_start(img[:, :, :], x[bass.ds(W.n * (PAIR * CH), PAIR * CH), :, :].rearrange(
                    "c h w -> h c w")).then_inc(img_in.sem, 16)

            def store(X):
                sp.wait_ge(*end_norm.of(X))
                sp.dma_start(out[bass.ds(X.n * TOK, TOK), :].rearrange("(k p) d -> p k d", p=128),
                             xe[:, :, :]).then_inc(out_done.sem, 16)

            def body(U, V, W, X):
                if W:
                    load_images(W)
                if X:
                    store(X)

            def epilogue(V, X):
                store(X)
                store(V)

            run_units(sp, load_images, body, epilogue)
            sp.wait_ge(out_done.sem, 16 * units)

        @block.tensor
        def _(pe):
            mm = nc.tensor.matmul
            rep_reader = [None]
            side_reader = [None]

            def side_banks(reader):
                if side_reader[0]:
                    pe.wait_ge(*side_reader[0])
                side_reader[0] = reader

            def transposes(src, banks, done):
                for c in range(KM):
                    for k in range(TILES):
                        last = nc.tensor.transpose(T[banks[c]][0:KC, k * 128:(k + 1) * 128],
                                                   src[:, k, c * KC:(c + 1) * KC], ident)
                    last.then_inc(done.sem, 1)

            def token_major(dst, k, pairs, signal):
                for n, (lhs, rhs) in enumerate(pairs):
                    last = mm(dst[:, k % 2, :], lhs, rhs, start=(n == 0), stop=(n == len(pairs) - 1))
                if k % 2:
                    last.then_inc(signal.sem, 1)

            def tok(k):
                return slice(k * 128, (k + 1) * 128)

            def outproj(V):
                side_banks(res_dve.of(V, 2))
                pe.wait_ge(*gated.of(V))
                for k in range(TILES):
                    token_major(two(k // 2), k, [(act1[:, c, tok(k)], wout[:, c, :]) for c in range(CI)], outproj_pe)

            def post_transpose(n, src, norm):
                def step(V):
                    side_banks(post_xT.of(V, KM * (n + 1)))
                    pe.wait_ge(*post_norm.of(V, TILES * norm))
                    transposes(src, (0, 1), post_tp)
                return step

            def ffn(V):
                side_banks(res_dve.of(V, 4))
                pe.wait_ge(*post_xT.of(V, KM))
                for k in range(TILES):
                    token_major(two(k // 2), k, [(xT[:, c, tok(k)], ffn_w[:, c, :]) for c in range(KM)], ffn_pe)

            def w_in_step(m):
                def step(V):
                    side_banks(w_in_act.of(V, m + 1))
                    if m == 0:
                        pe.wait_ge(*post_xT.of(V, 2 * KM))
                    for c in range(KM):
                        last = mm(T[m % 2][:, :], w_in[:, c, m * 128:(m + 1) * 128], xT[:, c, :],
                                  start=(c == 0), stop=(c == KM - 1))
                    last.then_inc(w_in_pe.sem, 1)
                return step

            def xd(V):
                side_banks(xd_act.of(V, 6))
                pe.wait_ge(*act1_dve.of(V))
                for c in range(CI):
                    last = mm(T[0][0:64, :], wdd[:, c, :], act1[:, c, :], start=(c == 0), stop=(c == CI - 1))
                last.then_inc(xd_pe.sem, 1)

            def w_out(V):
                side_banks(res_dve.of(V, 6))
                for k in range(TILES):
                    for c in range(CI):
                        mm(two(k // 2)[:, k % 2, :], act1[:, c, tok(k)], w_y[:, c, :],
                           start=(k % 2 == 0 and c == 0), stop=False, skip_group_check=True)
                pe.wait_ge(*states_dve.of(V))
                for k in range(TILES):
                    rows, cols = slice(32 * (k // 2), 32 * (k // 2) + 32), tok(k % 2)
                    last = mm(two(k // 2)[:, k % 2, :], s_v[rows, cols], w_us[rows, :], start=False, stop=(k % 2 == 1),
                              skip_group_check=True)
                    if k % 2:
                        last.then_inc(w_out_pe.sem, 1)

            def gate(V):
                side_banks(gate_act.of(V))
                pe.wait_ge(*post_xT.of(V))
                for k in range(TILES):
                    for c in range(KM):
                        last = mm(T[0][:, k * E:(k + 1) * E], xeT[:, c, tok(k)], gate_w[:, c, :],
                                  start=(c == 0), stop=(c == KM - 1))
                last.then_inc(gate_pe.sem, 1)

            def cw_transpose(V):
                side_banks(cwT_act.of(V))
                pe.wait_ge(*route_dve.of(V))
                for k in range(TILES):
                    last = nc.tensor.transpose(T[1][0:3 * E, tok(k)], cws[:, k, :], ident)
                last.then_inc(cwT_pe.sem, 1)

            def down(e):
                def step(X):
                    if e == 0 and X.has_previous:
                        pe.wait_ge(*res4_dve.before(X))
                    if e < E:
                        pe.wait_ge(*expert_scaled.of(X, e + 1))
                    else:
                        pe.wait_ge(*expert_hid.of(X))
                    for k in range(TILES):
                        last = mm(two(2 + k // 2)[:, k % 2, :], hid[:, tok(k)], w2[:, e, :],
                                  start=(e == 0 and k % 2 == 0), stop=(e == E), skip_group_check=True)
                    last.then_inc(expert_down.sem, 1)
                return step

            def expert(e):
                def step(X, U, W, b):
                    side_banks(expert_hid.of(X, 2 * e + 2))
                    if e == 0:
                        pe.wait_ge(*cwT_act.of(X))
                    for i, w in ((0, w1), (1, w3)):
                        for c in range(KM):
                            last = mm(T[i][:, :], w[:, c, e * INTER:(e + 1) * INTER], xeT[:, c, :],
                                      start=(c == 0), stop=(c == KM - 1))
                        last.then_inc(expert_up.sem, 1)
                    if e < E:
                        pe.wait_ge(*(rep_reader[0] or rep_done(U, W, b)))
                        mm(rep[:, :], sel_e_sb[:, e, :], cwT, start=True, stop=True).then_inc(crep_mm.sem, 1)
                        rep_reader[0] = crep_out.of(X, e + 1)
                return step

            def gather(W):
                side_banks(gather_dve.of(W))
                pe.wait_ge(*img_in.of(W))
                for ch in range(CH):
                    if ch == 2:
                        pe.wait_ge(*gather_dve.of(W, 1))
                    for b in range(PAIR):
                        last = mm(T[ch % 2][0:SIDE, b * L:(b + 1) * L], img[:, b * CH + ch, :], row_hot[:, :],
                                  start=True, stop=True)
                    last.then_inc(gather_pe.sem, 1)

            def embed(W):
                side_banks(embed_dve.of(W))
                pe.wait_ge(*gather_dve.of(W))
                for k in range(TILES):
                    token_major(two(k // 2), k, [(masked[:, ch, tok(k)], pw[:, ch, :]) for ch in range(CH)],
                                embed_pe)

            def x0T_step(W):
                side_banks(pre_xT.of(W))
                pe.wait_ge(*pre_norm.of(W))
                transposes(xn0, (0, 1), pre_tp)

            def xz(m):
                def step(W):
                    side_banks(gz_dve.of(W, m + 1))
                    if m == 0:
                        pe.wait_ge(*pre_xT.of(W))
                    for i in range(2):
                        for c in range(KM):
                            last = mm(T[i][:, :], win[:, c, i * DI + m * 128:i * DI + (m + 1) * 128], x0T[:, c, :],
                                      start=(c == 0), stop=(c == KM - 1))
                        last.then_inc(xz_pe.sem, 1)
                return step

            def bc(W):
                side_banks(bc_dve.of(W, 2))
                pe.wait_ge(*xc_dve.of(W))
                for i in range(2):
                    for c in range(CI):
                        last = mm(T[i][0:96, :], wx_bc[:, c, i * 96:(i + 1) * 96], xc[:, c, :],
                                  start=(c == 0), stop=(c == CI - 1))
                    last.then_inc(bc_pe.sem, 1)

            def delta_step(m):
                def step(W):
                    side_banks(abs_act.of(W, m + 1))
                    bank = m % 2
                    for c in range(CI):
                        last = mm(T[bank][:, :], wx_d[:, c, m * 128:(m + 1) * 128], xc[:, c, :],
                                  start=(c == 0), stop=(c == CI - 1))
                    last.then_inc(delta_pe.sem, 1)
                return step

            post = {"outproj": outproj, "x1T": post_transpose(0, xs, 1), "ffn": ffn, "xnT": post_transpose(1, xn1, 3),
                    **{f"conv1_{m}": w_in_step(m) for m in range(CI)}, "xd": xd, "w_out": w_out,
                    "x3T": post_transpose(2, xe, 4), "gate": gate, "cwT": cw_transpose}
            experts = {f"expert{e}": expert(e) for e in range(E + 1)}
            post.update({f"down{e}": down(e) for e in range(E + 1)})
            steps = {**post,
                   "gather": gather, "embed": embed, "x0T": x0T_step, "xz0": xz(0), "xz1": xz(1), "xz2": xz(2), "bc": bc,
                   "delta0": delta_step(0), "delta1": delta_step(1), "delta2": delta_step(2)}

            def replicate(unit, g, i, s):
                n = 4 * g + 2 * i + s
                if n == 0:
                    pe.wait_ge(*bc_dve.of(unit))
                if rep_reader[0]:
                    pe.wait_ge(*rep_reader[0])
                    rep_reader[0] = None
                elif n or unit.has_previous:
                    pe.wait_ge(*rep_out.of(unit, n))
                mm(rep[:, :], sel_sb[0:96, NG * g + s, :], bc_st[:, unit.parity, i, :], start=True,
                   stop=True).then_inc(rep_mm.sem, 1)

            def replicate_rows(U, W, b, when):
                unit, g = rep_target(U, W, b)
                for i, s in rep_jobs(b, when) if unit else ():
                    replicate(unit, g, i, s)

            def rep_done(U, W, b):
                n = 4 * (b // CI + 1) + sum(len(j) for j in REP_FRONT[:b % CI + 1] + REP_BEHIND[:b % CI])
                return rep_out.of(U, n if W else min(n, 4 * GROUPS))

            def add_up(U, b):
                g, c = b // CI, b % CI
                if g == 0:
                    if U.has_previous:
                        pe.wait_ge(*gated.before(U, c + 1))
                    mm(y[c][:, :], diag_d[:, c, :], xc[:, c, :], start=True, stop=False,
                       skip_group_check=True).then_inc(diag_in.sem, 1)
                pe.wait_ge(*weighted.of(U, b + 1))
                for s in range(NG):
                    last = mm(y[c][:, :], ident, drive[:, b % NX, s, :], start=False,
                              stop=(g == GROUPS - 1 and s == NG - 1), skip_group_check=True)
                last.then_inc(summed.sem, 1)

            def first_group(W):
                for i in range(2):
                    for s in range(NG):
                        replicate(W, 0, i, s)

            def prologue(W):
                pe.wait_ge(loaded, 6 * 16)
                for c in range(CI):
                    for i in range(KM):
                        last = mm(T[c][:, 0:DM], wxpT[:, i, c * 128:(c + 1) * 128], wo_y[:, i, :],
                                  start=(i == 0), stop=(i == KM - 1))
                    last.then_inc(setup_pe, 1)
                for i in range(KM):
                    last = mm(T[3][0:PAIR * 32, 0:DM], w_usT[:, i, :], wo_y[:, i, :], start=(i == 0), stop=(i == KM - 1))
                last.then_inc(setup_pe, 1)
                for n, (by, i) in enumerate((by, i) for by in (by1, by2) for i in range(KM)):
                    last = mm(T[3][:, DM:2 * DM], by[:, i, :], wo_y[:, i, :], start=(n == 0), stop=(n == 2 * KM - 1))
                last.then_inc(setup_pe, 1)
                pe.wait_ge(setup_dve, SETUP_DVE)
                pe.wait_ge(setup_act, SETUP_ACT)
                for s in sum(PRE, []):
                    if s in steps:
                        steps[s](W)
                first_group(W)

            def side(s, unit, U, W, b):
                if s in experts:
                    experts[s](unit, U, W, b)
                elif s in steps:
                    steps[s](unit)

            def body(U, V, W, X):
                if X:
                    side_reader[0] = last_side(X)
                for b in range(BLOCKS):
                    replicate_rows(U, W, b, "front")
                    for s, unit in sides(PLAN[b], V, W, X):
                        side(s, unit, U, W, b)
                    replicate_rows(U, W, b, "behind")
                    if b >= LAG:
                        add_up(U, b - LAG)
                    elif V:
                        add_up(V, BLOCKS + b - LAG)

            def last_side(X):
                e = sum(kind == "late" and s.startswith("expert") for b in PLAN for kind, s in PLAN[b]) - 1
                return expert_hid.of(X, 2 * e + 2)

            def epilogue(V, X):
                for b in range(BLOCKS - LAG, BLOCKS):
                    add_up(V, b)
                rep_reader[0] = rep_reader[0] or rep_out.of(V)
                for s, unit in rest(V, X):
                    side(s, unit, None, None, 0)

            run_units(pe, prologue, body, epilogue)

        @block.scalar
        def _(act):
            f = nc.scalar.activation

            def post_evacuate(n, scale=None, bias=None):
                def step(V):
                    for c in range(KM):
                        act.wait_ge(*post_tp.of(V, KM * n + c + 1))
                        if scale is None:
                            f((xeT if n == 2 else xT)[:, c, :], T[c][0:KC, :], ACT.Copy).then_inc(post_xT.sem, 1)
                        else:
                            f(xT[:, c, :], T[c][0:KC, :], ACT.Identity, scale=scale[:, c:c + 1],
                              bias=bias[:, c:c + 1]).then_inc(post_xT.sem, 1)
                return step

            def tanh_act1(V, m):
                act.wait_ge(*conv1_dve.of(V, TAPS1 * (m + 1)))
                if m:
                    act.wait_ge(*act1_dve.of(V, m))
                f(th1, act1[:, m, :], ACT.Tanh).then_inc(conv1_act.sem, 1)

            def conv1(m):
                def step(V):
                    act.wait_ge(*w_in_pe.of(V, m + 1))
                    f(convin1[:, m, :, TAPS1 - 1:], halves(T[m % 2][:, :]), ACT.Identity,
                      bias=b_in[:, m:m + 1]).then_inc(w_in_act.sem, 1)
                    if m:
                        tanh_act1(V, m - 1)
                return step

            def gate1(V):
                tanh_act1(V, CI - 1)

            def xd(V):
                act.wait_ge(*xd_pe.of(V))
                for b in range(PAIR):
                    rows, cols = slice(32 * b, 32 * b + 32), slice(b * L, (b + 1) * L)
                    f(s_e[rows], T[0][0:32, cols], ACT.Abs, bias=b_dt[rows]).then_inc(xd_act.sem, 1)
                    f(s_x[rows], T[0][0:32, cols], ACT.Identity, bias=b_dt[rows]).then_inc(xd_act.sem, 1)
                    f(s_ds[rows], T[0][32:64, cols], ACT.Identity, bias=b_ds[rows]).then_inc(xd_act.sem, 1)
                act.wait_ge(*xd_act.of(V, 6))
                f(s_e, s_e, ACT.Exp, scale=-1.0).then_inc(xd_act.sem, 1)
                act.wait_ge(*xd_act.of(V, 7))
                f(s_dt, s_e, ACT.Ln, bias=1.0).then_inc(xd_act.sem, 1)

            def decay_step(V):
                act.wait_ge(*dt_dve.of(V, 2))
                f(s_x, s_dt, ACT.Exp, scale=-1.0).then_inc(decay_act.sem, 1)
                f(s_e, s_dt, ACT.Exp, scale=-0.5).then_inc(decay_act.sem, 1)
                act.wait_ge(*dt_dve.of(V))
                f(s_p, s_k, ACT.Exp, scale=-1.0).then_inc(decay_act.sem, 1)
                f(s_t, s_dt, ACT.Tanh, scale=0.5).then_inc(decay_act.sem, 1)
                f(s_k, s_k, ACT.Tanh, scale=0.5).then_inc(decay_act.sem, 1)

            def gate(V):
                act.wait_ge(*gate_pe.of(V))
                f(r_score, T[0][:, 0:TILES * E], ACT.Tanh, scale=0.5).then_inc(gate_act.sem, 1)

            def cw_transpose(V):
                act.wait_ge(*cwT_pe.of(V))
                f(cwT, T[1][0:3 * E, :], ACT.Copy).then_inc(cwT_act.sem, 1)

            def expert(e):
                def step(X):
                    act.wait_ge(*expert_up.of(X, 2 * e + 1))
                    if e:
                        act.wait_ge(*expert_down.of(X, e))
                    elif X.has_previous:
                        act.wait_ge(*expert_down.before(X))
                    f(hid, T[0][:, :], ACT.Tanh).then_inc(expert_tanh.sem, 1)
                    if e < E:
                        act.wait_ge(*crep_mm.of(X, e + 1))
                        f(crep[:, :], rep[:, :], ACT.Copy).then_inc(crep_out.sem, 1)
                return step

            def x0T_step(W):
                act.wait_ge(*pre_tp.of(W))
                for c in range(KM):
                    f(x0T[:, c, :], T[c][0:KC, :], ACT.Identity, scale=g0[:, c:c + 1],
                      bias=b0[:, c:c + 1]).then_inc(pre_xT.sem, 1)

            def tanh_xc(W, m):
                act.wait_ge(*conv0_dve.of(W, TAPS0 * (m + 1)))
                if m:
                    act.wait_ge(*xc_dve.of(W, m))
                f(thc, xc[:, m, :], ACT.Tanh).then_inc(conv0_act.sem, 1)

            def xz(m):
                def step(W):
                    act.wait_ge(*xz_pe.of(W, 2 * m + 1))
                    if m:
                        act.wait_ge(*conv0_dve.of(W, TAPS0 * m))
                    f(convin0[:, :, PAD:], halves(T[0][:, :]), ACT.Copy).then_inc(convin0_act.sem, 1)
                    act.wait_ge(*xz_pe.of(W, 2 * m + 2))
                    f(thz, T[1][:, :], ACT.Tanh).then_inc(thz_act.sem, 1)
                    if m:
                        tanh_xc(W, m - 1)
                return step

            def xc_end(W):
                tanh_xc(W, CI - 1)

            def bc(W):
                for i in range(2):
                    act.wait_ge(*bc_pe.of(W, i + 1))
                    f(hi16[:, i, :], T[i][0:96, :], ACT.Copy).then_inc(bc_act.sem, 1)

            def bc_low(W):
                for i in range(2):
                    act.wait_ge(*bc_dve.of(W, i + 1))
                    f(hi16[:, i, :], low[:, i, :], ACT.Copy).then_inc(bc_act.sem, 1)

            def delta_step(m):
                def step(W):
                    if m == 0:
                        act.wait_ge(*bc_dve.of(W))
                    act.wait_ge(*delta_pe.of(W, m + 1))
                    f(delta[:, W.parity, m, :], T[m % 2][:, :], ACT.Relu).then_inc(relu_act.sem, 1)
                    f(soft_e[:, m, :], T[m % 2][:, :], ACT.Abs).then_inc(abs_act.sem, 1)
                    act.wait_ge(*abs_act.of(W, m + 1))
                    f(soft_e[:, m, :], soft_e[:, m, :], ACT.Exp, scale=-1.0).then_inc(exp_act.sem, 1)
                return step

            def soft(W):
                act.wait_ge(*exp_act.of(W))
                f(du[:, W.parity], soft_e, ACT.Ln, bias=1.0).then_inc(ln_act.sem, 1)

            post = {"x1T": post_evacuate(0), "xnT": post_evacuate(1, g1, b1), "gate1": gate1,
                    **{f"conv1_{m}": conv1(m) for m in range(CI)}, "xd": xd, "decay": decay_step, "x3T": post_evacuate(2), "gate": gate,
                    "cwT": cw_transpose, **{f"expert{e}": expert(e) for e in range(E + 1)}}
            steps = {**post,
                   "x0T": x0T_step, "xz0": xz(0), "xz1": xz(1), "xz2": xz(2), "xc_end": xc_end, "bc": bc,
                   "bc_low": bc_low, "delta0": delta_step(0), "delta1": delta_step(1), "delta2": delta_step(2),
                   "soft": soft}

            def copy_rep(unit, g, i, s):
                n = 4 * g + 2 * i + s
                act.wait_ge(*rep_mm.of(unit, n + 1))
                if g >= 2 or unit.has_previous:
                    act.wait_ge(*(weighted if i else scanned).of(unit, CI * (g - 1)))
                f(bc_rep[:, g % 2, i, s, :], rep[:, :], ACT.Copy).then_inc(rep_out.sem, 1)

            def copy_rows(U, W, b, when):
                unit, g = rep_target(U, W, b)
                for i, s in rep_jobs(b, when) if unit else ():
                    copy_rep(unit, g, i, s)

            def decays(U, b):
                g, c = b // CI, b % CI
                if b == 0:
                    act.wait_ge(*delta_dve.of(U))
                if b >= NA or U.has_previous:
                    act.wait_ge(*scanned.of(U, b + 1 - NA))
                for s in range(NG):
                    n = NG * g + s
                    last = f(halves(decay[:, b % NA, s, :])[:, :, 1:], halves(delta[:, U.parity, c, :])[:, :, 1:],
                             ACT.Exp, scale=a_neg[:, c, n:n + 1])
                last.then_inc(decay_ready.sem, 1)

            def prologue(W):
                act.wait_ge(loaded, 6 * 16)
                al = w128[:, W128["a_log"][0]:W128["a_log"][0] + CI * DS]
                act.wait_ge(setup_dve, 3)
                f(al, al, ACT.Exp).then_inc(setup_act, 1)
                fw = w96[:, W96["ffn"][0]:W96["ffn"][0] + KM * DM]
                f(fw, fw, ACT.Sign).then_inc(setup_act, 1)
                act.wait_ge(setup_dve, SETUP_DVE)
                for s in sum(PRE, []):
                    if s in steps:
                        steps[s](W)
                for i in range(2):
                    for s in range(NG):
                        copy_rep(W, 0, i, s)

            def body(U, V, W, X):
                for b in range(BLOCKS):
                    decays(U, b)
                    copy_rows(U, W, b, "front")
                    for s, unit in sides(PLAN[b], V, W, X):
                        if s in steps:
                            steps[s](unit)
                    copy_rows(U, W, b, "behind")

            def epilogue(V, X):
                for s, unit in rest(V, X):
                    if s in steps:
                        steps[s](unit)

            run_units(act, prologue, body, epilogue)

        @block.vector
        def _(dve):
            v = nc.vector

            def norm_stats(unit, src, stat, before, own=(stats, mv)):
                for k in range(TILES):
                    v.bn_stats(own[0][:, k, :], src[:, k, :]).then_inc(stat.sem, 1)
                dve.wait_ge(*stat.of(unit, before + TILES))
                v.memset(spare[:, 0:1], 0.0)
                for k in range(TILES):
                    v.bn_aggr(own[1][:, k, :], own[0][:, k, :]).then_inc(stat.sem, 1)

            def norm_apply(unit, dst, src, rst, norm, n, own=(mv, rstd)):
                dve.wait_ge(*rst.of(unit, 2 * n + 2))
                for k in range(TILES):
                    v.tensor_scalar(dst[:, k, :], src[:, k, :], own[0][:, k, 0:1], own[1][:, k:k + 1], ALU.subtract,
                                    ALU.mult).then_inc(norm.sem, 1)

            def res1(V):
                for b in range(2):
                    dve.wait_ge(*outproj_pe.of(V, b + 1))
                    v.scalar_tensor_tensor(xs[:, 2 * b:2 * b + 2, :], h0[:, V.parity, 2 * b:2 * b + 2, :], 2.0,
                                           two(b), ALU.mult, ALU.add).then_inc(res_dve.sem, 1)
                dve.wait_ge(*res_dve.of(V, 2))
                norm_stats(V, xs, post_stats, 0)

            def residual(n, pe_signal, bank, stat):
                def step(V):
                    if n == 3:
                        dve.wait_ge(*bias_pool.of(V))
                    for b in range(2):
                        dve.wait_ge(*pe_signal.of(V, b + 1))
                        v.tensor_tensor(xs[:, 2 * b:2 * b + 2, :], xs[:, 2 * b:2 * b + 2, :], two(bank + b),
                                        ALU.add).then_inc(res_dve.sem, 1)
                    dve.wait_ge(*res_dve.of(V, 2 * n))
                    norm_stats(V, xs, post_stats, 8 * stat)
                return step

            def res4(X):
                dve.wait_ge(*expert_down.of(X))
                for b in range(2):
                    v.tensor_tensor(xe[:, 2 * b:2 * b + 2, :], xe[:, 2 * b:2 * b + 2, :], two(2 + b),
                                    ALU.add).then_inc(res4_dve.sem, 1)
                dve.wait_ge(*res4_dve.of(X))
                norm_stats(X, xe, end_stats, 0, (stats4, mv4))

            def norm4(X):
                norm_apply(X, xe, xe, end_rstd, end_norm, 0, (mv4, rstd4))

            def norm(n, dst):
                def step(V):
                    if n == 3 and V.has_previous:
                        dve.wait_ge(*out_done.before(V))
                    norm_apply(V, dst, xs, post_rstd, post_norm, n)
                    if n == 1:
                        dve.wait_ge(*post_norm.of(V, 2 * TILES))
                        norm_stats(V, xs, post_stats, 16)
                    if n == 2:
                        v.memset(convin1[:, :, :, 0:TAPS1 - 1], 0.0).then_inc(pad_dve.sem, 1)
                return step

            def gate_act1(V, m):
                dve.wait_ge(*conv1_act.of(V, m + 1))
                v.scalar_tensor_tensor(act1[:, m, :], th1, 1.0, act1[:, m, :], ALU.add,
                                       ALU.mult).then_inc(act1_dve.sem, 1)

            def conv1(m):
                def step(V):
                    if m == 0:
                        dve.wait_ge(*pad_dve.of(V))
                    dve.wait_ge(*w_in_act.of(V, m + 1))
                    for t in range(TAPS1):
                        src, w, n = convin1[:, m, :, t:t + L], cw1[:, m, t:t + 1], TAPS1 * m + t
                        if t == 0:
                            v.tensor_scalar(halves(act1[:, m, :]), src, w, cb1[:, m:m + 1], ALU.mult,
                                            ALU.add).then_inc(conv1_dve.sem, 1)
                        else:
                            dve.wait_ge(*conv1_dve.of(V, n))
                            v.scalar_tensor_tensor(halves(act1[:, m, :]), src, w, halves(act1[:, m, :]), ALU.mult,
                                                   ALU.add).then_inc(conv1_dve.sem, 1)
                    if m:
                        gate_act1(V, m - 1)
                return step

            def gate1(V):
                gate_act1(V, CI - 1)

            def dt_step(V):
                dve.wait_ge(*xd_act.of(V))
                v.scalar_tensor_tensor(s_dt, s_e, 0.69, s_dt, ALU.mult, ALU.max).then_inc(dt_dve.sem, 1)
                dve.wait_ge(*dt_dve.of(V, 1))
                v.scalar_tensor_tensor(s_dt, s_x, 0.0, s_dt, ALU.max, ALU.add).then_inc(dt_dve.sem, 1)
                dve.wait_ge(*dt_dve.of(V, 2))
                v.tensor_tensor(s_k, s_dt, ktab, ALU.mult).then_inc(dt_dve.sem, 1)

            def states_step(V):
                n = [0]

                def then(ins):
                    n[0] += 1
                    ins.then_inc(states_dve.sem, 1)
                    dve.wait_ge(*states_dve.of(V, n[0]))

                dve.wait_ge(*decay_act.of(V))
                then(v.tensor_tensor(s_ds, s_ds, s_e, ALU.mult))
                then(v.tensor_tensor_scan(s_v, s_x, s_ds, 0.0, ALU.mult, ALU.add))
                then(v.tensor_tensor(s_v, s_p, s_v, ALU.mult))
                then(v.scalar_tensor_tensor(s_k, s_p, 1.0, s_k, ALU.add, ALU.mult))
                then(v.scalar_tensor_tensor(s_x, s_x, 1.0, s_t, ALU.add, ALU.mult))
                then(v.tensor_scalar(s_x, s_x, 1e-30, None, ALU.max))
                then(v.reciprocal(s_x, s_x))
                then(v.tensor_tensor(s_k, s_k, s_x, ALU.mult))
                then(v.tensor_tensor(s_k, s_k, s_ds, ALU.mult))
                then(v.tensor_tensor(s_v, s_v, s_k, ALU.add))

            G = E // 2

            def router(V, n):
                n = [n]

                def then(ins):
                    n[0] += 1
                    ins.then_inc(route_dve.sem, 1)
                    dve.wait_ge(*route_dve.of(V, n[0]))
                return then

            def wide(ap, a, b, axis):
                return ap.unsqueeze(axis).broadcast_to([128, TILES, a, b])

            def route0(V):
                then = router(V, 0)
                dve.wait_ge(*gate_act.of(V))
                then(v.tensor_scalar(r_score, r_score, 0.5, 0.5, ALU.mult, ALU.add))
                s3 = r_s.rearrange("p (k e) -> p k e", e=E)
                then(v.tensor_tensor(s3, r_score.rearrange("p (k e) -> p k e", e=E),
                                     gbias.unsqueeze(1).broadcast_to([128, TILES, E]), ALU.add))
                then(v.tensor_tensor(r_g, r_s[:, 0::2], r_s[:, 1::2], ALU.add))
                then_rank(then, r_g.rearrange("p (k g) -> p k g", g=G), G, lt4, r_gsel)
                then(v.tensor_scalar(r_off, r_gsel, BIG, -BIG, ALU.mult, ALU.add))

            def route1(V):
                then = router(V, 10)
                pair = [128, TILES * G, 2]
                m3 = r_m.rearrange("p (g e) -> p g e", e=2)
                then(v.tensor_tensor(m3, r_s.rearrange("p (g e) -> p g e", e=2),
                                     r_gsel.unsqueeze(2).broadcast_to(pair), ALU.mult))
                then(v.tensor_tensor(m3, m3, r_off.unsqueeze(2).broadcast_to(pair), ALU.add))
                then_rank(then, r_m.rearrange("p (k e) -> p k e", e=E), E, lt8, r_sel)

            def route2(V):
                then = router(V, 18)
                then(v.tensor_tensor(r_cw, r_score, r_sel, ALU.mult))
                then(v.tensor_reduce(r_sum, r_cw.rearrange("p (k e) -> p k e", e=E), AX.X, ALU.add))
                then(v.tensor_scalar(r_sum, r_sum, 1e-6, None, ALU.add))
                then(v.reciprocal(r_sum, r_sum))
                c3 = r_cw.rearrange("p (k e) -> p k e", e=E)
                then(v.tensor_tensor(c3, c3, r_sum.unsqueeze(2).broadcast_to([128, TILES, E]), ALU.mult))
                h3 = hb[:, :].rearrange("p (k e) -> p k e", e=E)
                then(v.tensor_copy(h3, c3))
                then(v.tensor_copy(cws[:, :, 0:E], h3))
                then(v.tensor_tensor(c3, c3, h3, ALU.subtract))
                then(v.tensor_copy(h3, c3))
                then(v.tensor_copy(cws[:, :, E:2 * E], h3))
                then(v.tensor_tensor(cws[:, :, 2 * E:3 * E], c3, h3, ALU.subtract))

            def then_rank(then, val, n, lower, dst):
                me, other = wide(val, n, n, 3), wide(val, n, n, 2)
                gt = r_gt[:, 0:TILES * n * n].rearrange("p (k a b) -> p k a b", a=n, b=n)
                eq = r_eq[:, 0:TILES * n * n].rearrange("p (k a b) -> p k a b", a=n, b=n)
                then(v.tensor_tensor(gt, other, me, ALU.is_gt))
                then(v.tensor_tensor(eq, other, me, ALU.is_equal))
                then(v.tensor_tensor(eq, eq, lower.unsqueeze(1).broadcast_to([128, TILES, n, n]), ALU.mult))
                then(v.tensor_tensor(gt, gt, eq, ALU.add))
                then(v.tensor_reduce(dst.rearrange("p (k a) -> p k a", a=n), gt, AX.X, ALU.add))
                then(v.tensor_scalar(dst, dst, 2.0, None, ALU.is_lt))

            def expert(e):
                def step(X):
                    dve.wait_ge(*expert_tanh.of(X, e + 1))
                    v.scalar_tensor_tensor(hid, hid, 1.0, T[0][:, :], ALU.add, ALU.mult).then_inc(expert_hid.sem, 1)
                    dve.wait_ge(*expert_up.of(X, 2 * e + 2))
                    dve.wait_ge(*expert_hid.of(X, 2 * e + 1))
                    v.tensor_tensor(hid, hid, T[1][:, :], ALU.mult).then_inc(expert_hid.sem, 1)
                return step

            def gather(W):
                for ch in range(CH):
                    dve.wait_ge(*gather_pe.of(W, ch + 1))
                    v.tensor_tensor(halves(masked[:, ch, :]), halves(T[ch % 2][0:SIDE, :]), twice(col_hot[:, :]),
                                    ALU.mult).then_inc(gather_dve.sem, 1)

            def embed(W):
                for b in range(2):
                    dve.wait_ge(*embed_pe.of(W, b + 1))
                    v.tensor_tensor(h0[:, W.parity, 2 * b:2 * b + 2, :], two(b),
                                    pb.unsqueeze(1).broadcast_to([128, 2, DM]), ALU.add).then_inc(embed_dve.sem, 1)
                dve.wait_ge(*embed_dve.of(W))
                norm_stats(W, h0[:, W.parity], pre_stats, 0, (stats0, mv0))

            def norm0(W):
                norm_apply(W, xn0, h0[:, W.parity], pre_rstd, pre_norm, 0, (mv0, rstd0))

            def xc_gate(W, m):
                dve.wait_ge(*conv0_act.of(W, m + 1))
                v.scalar_tensor_tensor(xc[:, m, :], thc, 1.0, xc[:, m, :], ALU.add,
                                       ALU.mult).then_inc(xc_dve.sem, 1)

            def conv0(W, m, taps):
                for t in taps:
                    src, w = convin0[:, :, t:t + L], cw0[:, m, t:t + 1]
                    if t == 0:
                        v.tensor_scalar(halves(xc[:, m, :]), src, w, cb0[:, m:m + 1], ALU.mult,
                                        ALU.add).then_inc(conv0_dve.sem, 1)
                    else:
                        dve.wait_ge(*conv0_dve.of(W, TAPS0 * m + t))
                        v.scalar_tensor_tensor(halves(xc[:, m, :]), src, w, halves(xc[:, m, :]), ALU.mult,
                                               ALU.add).then_inc(conv0_dve.sem, 1)

            def xz(m):
                def step(W):
                    if m == 0 and W.has_previous:
                        dve.wait_ge(*diag_in.before(W))
                        dve.wait_ge(*delta_pool.before(W))
                    dve.wait_ge(*convin0_act.of(W, m + 1))
                    conv0(W, m, range(TAPS_A))
                    dve.wait_ge(*thz_act.of(W, m + 1))
                    v.scalar_tensor_tensor(gz[:, W.parity, m, :], thz, 1.0, T[1][:, :], ALU.add,
                                           ALU.mult).then_inc(gz_dve.sem, 1)
                return step

            def conv0_end(m):
                def step(W):
                    conv0(W, m, range(TAPS_A, TAPS0))
                    if m:
                        xc_gate(W, m - 1)
                return step

            def xc_end(W):
                xc_gate(W, CI - 1)

            def bc(W):
                for i in range(2):
                    dve.wait_ge(*bc_act.of(W, i + 1))
                    v.scalar_tensor_tensor(low[:, i, :], hi16[:, i, :], m1, T[i][0:96, :], ALU.mult,
                                           ALU.add).then_inc(bc_dve.sem, 1)

            def bc_low(W):
                for i in range(2):
                    dve.wait_ge(*bc_act.of(W, i + 3))
                    v.scalar_tensor_tensor(bc_st[:, W.parity, i, :], hi16[:, i, :], m2, low[:, i, :], ALU.mult,
                                           ALU.add).then_inc(bc_dve.sem, 1)

            def soft(W):
                lg = du[:, W.parity]
                dve.wait_ge(*ln_act.of(W))
                v.scalar_tensor_tensor(lg, soft_e, 0.69, lg, ALU.mult, ALU.max).then_inc(delta_dve.sem, 1)
                dve.wait_ge(*delta_dve.of(W, 1))
                v.tensor_tensor(delta[:, W.parity], delta[:, W.parity], lg, ALU.add).then_inc(delta_dve.sem, 1)

            post = {"res1": res1, "norm1": norm(0, xs), "res2": residual(2, ffn_pe, 0, 1), "norm2": norm(1, xs),
                    "prenorm": norm(2, xn1), "gate1": gate1,
                    **{f"conv1_{m}": conv1(m) for m in range(CI)}, "dt": dt_step, "states": states_step,
                    "res3": residual(3, w_out_pe, 0, 3), "norm3": norm(3, xe), "route0": route0, "route1": route1, "route2": route2,
                    "res4": res4, "norm4": norm4,
                    **{f"expert{e}": expert(e) for e in range(E + 1)}}
            steps = {**post,
                   "gather": gather, "embed": embed, "norm0": norm0, **{f"xz{m}": xz(m) for m in range(CI)},
                   **{f"conv0_{m}": conv0_end(m) for m in range(CI)}, "xc_end": xc_end, "bc": bc, "bc_low": bc_low,
                   "soft": soft}

            def scan(U, b):
                g, c = b // CI, b % CI
                mine, pools = drives(b)
                if on_pool(b):
                    dve.wait_ge(*drive_pool.of(U, pools))
                else:
                    dve.wait_ge(*rep_out.of(U, 4 * g + 2))
                    if b < CI:
                        dve.wait_ge(*delta_pool.of(U))
                    if b >= NX or U.has_previous:
                        dve.wait_ge(*summed.of(U, b + 1 - NX))
                    v.tensor_tensor(drive[:, b % NX], du[:, U.parity, c, :].unsqueeze(1).broadcast_to([128, NG, TOK]),
                                    bc_rep[:, g % 2, 0], ALU.mult).then_inc(drive_dve.sem, 1)
                    dve.wait_ge(*drive_dve.of(U, mine))
                dve.wait_ge(*decay_ready.of(U, b + 1))
                flat = drive[:, b % NX].rearrange("p s t -> p (s t)")
                v.tensor_tensor_scan(flat, decay[:, b % NA].rearrange("p s t -> p (s t)"), flat, 0.0, ALU.mult,
                                     ALU.add).then_inc(scanned.sem, 1)

            def tail(V, c):
                dve.wait_ge(*summed.of(V, BLOCKS - CI + c + 1))
                v.tensor_tensor(act1[:, c, :], y[c][:, :], gz[:, V.parity, c, :], ALU.mult).then_inc(gated.sem, 1)

            def prologue(W):
                n = [0]

                def setup(ins):
                    n[0] += 1
                    ins.then_inc(setup_dve, 1)

                setup(v.memset(decay[:, :, :, :], 0.0))
                setup(v.memset(convin0[:, :, :], 0.0))
                dve.wait_ge(loaded, 6 * 16)
                al = w128[:, W128["a_log"][0]:W128["a_log"][0] + CI * DS]
                setup(v.tensor_scalar(al, al, LOG_MAX, None, ALU.min))
                setup(v.tensor_scalar(row_hot[:, :], curve_i[:, 1, :], part, None, ALU.is_equal))
                setup(v.tensor_scalar(col_hot[:, :], curve_i[:, 0, :], part, None, ALU.is_equal))
                for name, w in (("cw0", CI * TAPS0), ("cb0", CI), ("cw1", CI * TAPS1), ("cb1", CI)):
                    ap = w128[:, W128[name][0]:W128[name][0] + w]
                    setup(v.tensor_scalar(ap, ap, 0.5, None, ALU.mult))
                setup(v.tensor_scalar(win[:, :, DI:], win[:, :, DI:], 0.5, None, ALU.mult))
                setup(v.tensor_scalar(w1, w1, 0.5, None, ALU.mult))
                for c in range(CI):
                    setup(v.tensor_scalar(diag_d[:, c, :], ident, dskip[:, c:c + 1], None, ALU.mult))
                dve.wait_ge(setup_pe, CI + 2)
                for c in range(CI):
                    setup(v.tensor_tensor(w_y[:, c, :], w_y[:, c, :], T[c][:, 0:DM], ALU.add))
                setup(v.tensor_copy(w_us[:, :], T[3][0:PAIR * 32, 0:DM]))
                setup(v.tensor_tensor(b_out, b_out, T[3][:, DM:2 * DM], ALU.add))
                dve.wait_ge(setup_act, 1)
                setup(v.tensor_scalar(al, al, -1.0, None, ALU.mult))
                assert n[0] == SETUP_DVE
                dve.wait_ge(setup_dve, SETUP_DVE)
                for s in sum(PRE, []):
                    if s in steps:
                        steps[s](W)

            def body(U, V, W, X):
                for b in range(BLOCKS):
                    scan(U, b)
                    for c in range(CI):
                        if b == TAIL_AT[c] and V:
                            tail(V, c)
                    for s, unit in sides(PLAN[b], V, W, X):
                        if s in steps:
                            steps[s](unit)

            def epilogue(V, X):
                for c in range(CI):
                    tail(V, c)
                for s, unit in rest(V, X):
                    if s in steps:
                        steps[s](unit)

            run_units(dve, prologue, body, epilogue)

        @block.gpsimd
        def _(pool):
            g_ = nc.gpsimd

            def rstd_step(n, stat, rst, own=(mv, rstd)):
                def step(unit):
                    pool.wait_ge(*stat.of(unit, 8 * (n + 1)))
                    g_.tensor_tensor(own[1][:, :], own[0][:, :, 1], eps, ALU.add).then_inc(rst.sem, 1)
                    pool.wait_ge(*rst.of(unit, 2 * n + 1))
                    g_.tensor_tensor(own[1][:, :], own[1][:, :], half, ALU.pow).then_inc(rst.sem, 1)
                return step

            def output_bias(V):
                pool.wait_ge(*post_norm.of(V, 3 * TILES))
                g_.tensor_tensor(xs[:, :, :], xs[:, :, :], b_out.unsqueeze(1).broadcast_to([128, TILES, DM]),
                                 ALU.add).then_inc(bias_pool.sem, 1)

            def expert(e):
                def step(X):
                    pool.wait_ge(*expert_hid.of(X, 2 * e + 2))
                    pool.wait_ge(*crep_out.of(X, e + 1))
                    g_.tensor_tensor(hid, hid, crep[:, :], ALU.mult).then_inc(expert_scaled.sem, 1)
                return step

            def soft(W):
                pool.wait_ge(*delta_dve.of(W))
                for m in range(CI):
                    g_.tensor_tensor(du[:, W.parity, m, :], delta[:, W.parity, m, :], xc[:, m, :],
                                     ALU.mult).then_inc(delta_pool.sem, 1)

            post = {"res1": rstd_step(0, post_stats, post_rstd), "res2": rstd_step(1, post_stats, post_rstd),
                    "norm2": rstd_step(2, post_stats, post_rstd), "res3": rstd_step(3, post_stats, post_rstd),
                    "res4": rstd_step(0, end_stats, end_rstd, (mv4, rstd4)), "gate1": output_bias, **{f"expert{e}": expert(e) for e in range(E)}}
            steps = {**post,
                   "embed": rstd_step(0, pre_stats, pre_rstd, (mv0, rstd0)), "soft": soft}

            def drive_block(U, b):
                g, c = b // CI, b % CI
                pool.wait_ge(*rep_out.of(U, 4 * g + 2))
                if b < CI:
                    pool.wait_ge(*delta_pool.of(U))
                if b >= NX or U.has_previous:
                    pool.wait_ge(*summed.of(U, b + 1 - NX))
                g_.tensor_tensor(drive[:, b % NX], du[:, U.parity, c, :].unsqueeze(1).broadcast_to([128, NG, TOK]),
                                 bc_rep[:, g % 2, 0], ALU.mult).then_inc(drive_pool.sem, 1)

            def weigh(U, b):
                pool.wait_ge(*scanned.of(U, b + 1))
                pool.wait_ge(*rep_out.of(U, 4 * (b // CI) + 4))
                g_.tensor_tensor(drive[:, b % NX], drive[:, b % NX], bc_rep[:, (b // CI) % 2, 1],
                                 ALU.mult).then_inc(weighted.sem, 1)

            def prologue(W):
                pool.wait_ge(setup_dve, SETUP_DVE)
                for s in sum(PRE, []):
                    if s in steps:
                        steps[s](W)

            def body(U, V, W, X):
                for b in range(BLOCKS):
                    if b + 1 < BLOCKS and on_pool(b + 1):
                        drive_block(U, b + 1)
                    weigh(U, b)
                    for s, unit in sides(PLAN[b], V, W, X):
                        if s in steps:
                            steps[s](unit)

            def epilogue(V, X):
                for s, unit in rest(V, X):
                    if s in steps:
                        steps[s](unit)

            run_units(pool, prologue, body, epilogue)


def pack(parts, layout, width, rows):
    packed = np.zeros((rows, width), np.float32)
    for name, a in parts.items():
        start, w = layout[name]
        a = a.reshape(a.shape[0], -1)
        assert a.shape[1] == w, (name, a.shape, w)
        packed[:a.shape[0], start:start + w] = a
    return packed


def chunks(w, rows):
    return w.reshape(w.shape[0] // rows, rows, -1).transpose(1, 0, 2)


def per_channel(a, rows):
    return a.reshape(a.shape[0] // rows, rows, -1).transpose(1, 0, 2)


def layout(i):
    wx = i["L0_attn_Wx"].T
    bc = np.concatenate([wx[:, 0:DS]] * 3 + [wx[:, DS:2 * DS]] * 3, axis=1)
    wo = i["L1_attn_W_out"]
    w_y = np.concatenate([np.zeros((DM, DM), np.float32), wo[DM:DI]])
    pad = lambda w: np.concatenate([w, np.zeros((w.shape[0], 32 - N16), np.float32)], 1)
    images = lambda a: np.concatenate([a, np.zeros((32 - N16, a.shape[1]), np.float32)] * PAIR, 0)
    up = lambda w, s: np.concatenate([w, s[None]], 0).transpose(2, 0, 1).reshape(DM, -1)
    w2 = np.concatenate([i["L1_ffn_w2"], i["L1_ffn_sw2"][None]], 0).transpose(2, 0, 1)
    third = np.arange(96) // DS
    earlier = lambda n: np.tril(np.ones((n, n), np.float32), -1)
    rows = lambda a, n: np.broadcast_to(np.asarray(a, np.float32).reshape(1, -1), (n, np.asarray(a).size))
    p128 = pack({
        "ident": np.eye(128), "wx_bc": chunks(bc, 128), "wx_d": chunks(wx[:, 2 * DS:], 128),
        "wout": chunks(i["L0_attn_Wout"].T, 128), "w_y": chunks(w_y, 128),
        "wdd": chunks(np.concatenate([pad(i["L1_attn_W_dt"]), pad(i["L1_attn_W_xp"][:, DM:])], 1), 128), "w2": w2,
        "a_log": per_channel(i["L0_attn_A_log"], 128), "cw0": per_channel(i["L0_attn_conv_w"][:, 0], 128),
        "cb0": per_channel(i["L0_attn_conv_b"], 128), "dskip": per_channel(i["L0_attn_D"], 128),
        "b_in": per_channel(i["L1_attn_b_in"], 128), "cw1": per_channel(i["L1_attn_W_conv"][:, 0], 128),
        "cb1": per_channel(i["L1_attn_b_conv"], 128), "part": np.arange(128)[:, None],
        "m1": np.where(third >= 1, -1, 0)[:, None], "m2": np.where(third >= 2, -1, 0)[:, None],
        "pw": rows(i["L0_tok_proj_w"].T, SIDE), "pb": rows(i["L0_tok_proj_b"], 128),
        "gbias": rows(i["L1_ffn_gate_bias"], 128), "b_out": rows(i["L1_attn_b_out"], 128),
        "b_dt": images(i["L1_attn_b_dt"][:, None]), "b_ds": images(i["L1_attn_b_xp"][DM:, None]),
        "k": rows(np.arange(L - 1, -1, -1), 64), "lt4": rows(earlier(4), 128), "lt8": rows(earlier(8), 128),
        "half": np.full((128, TILES), -0.5), "eps": np.full((128, TILES), EPS)}, W128, N128, 128)
    p96 = pack({
        "win": chunks(i["L0_attn_Win"].T, KC), "ffn": chunks(i["L0_ffn_weight"].T, KC),
        "w_in": chunks(i["L1_attn_W_in"], KC),
        "gate": chunks(i["L1_ffn_gate_weight"].T, KC), "w1": chunks(up(i["L1_ffn_w1"], i["L1_ffn_sw1"]), KC),
        "w3": chunks(up(i["L1_ffn_w3"], i["L1_ffn_sw3"]), KC), "g0": per_channel(i["L0_attn_ln_g"], KC),
        "b0": per_channel(i["L0_attn_ln_b"], KC), "g1": per_channel(i["L1_attn_ln_g"], KC),
        "b1": per_channel(i["L1_attn_ln_b"], KC)}, W96, N96, KC)
    over_columns = lambda b: np.broadcast_to(b[:, None], (DM, 128))
    fold = pack({"wxpT": chunks(i["L1_attn_W_xp"][:, 0:DM].T, KC), "w_usT": chunks(images(i["L1_attn_W_us"]).T, KC),
                 "by1": chunks(over_columns(i["L1_attn_b_xp"][0:DM]), KC),
                 "by2": chunks(over_columns(i["L1_attn_b_us"]), KC), "wo_y": chunks(wo[0:DM], KC)}, FOLD, NFOLD, KC)
    bf = _mybir_np(BF16)
    one_of = lambda n: np.repeat(np.tile(np.eye(n, dtype=np.float32), (3, 1)), 128, axis=1).astype(bf)
    return {"x": i["x"].reshape(IMAGES * CH, SIDE, SIDE), "curve": np.ascontiguousarray(i["L0_tok_curve"].T),
            "p128": p128, "p96": p96, "fold": fold, "sel": one_of(DS), "sel_e": one_of(E)}


def _mybir_np(dt):
    return mybir.dt.np(dt)


def declare(nc, arrays, units=UNITS):
    aps = [nc.dram_tensor(f"in_{n}", a.shape, mybir.dt.from_np(a.dtype), kind="ExternalInput").ap()
           for n, a in arrays.items()]
    out = nc.dram_tensor("result", (IMAGES * L, DM), F32, kind="ExternalOutput").ap()
    build(nc, *aps, out, units=units)


def kernel(**inputs):
    import concourse.bacc as bacc
    from concourse.bass_utils import run_bass_kernel_spmd

    arrays = layout({k: np.asarray(a) for k, a in inputs.items()})
    nc = bacc.Bacc("TRN2", target_bir_lowering=False, num_devices=1)
    declare(nc, arrays)
    got = run_bass_kernel_spmd(nc, [{f"in_{n}": a for n, a in arrays.items()}], core_ids=[0])
    return got.results[0]["result"].reshape(IMAGES, L, DM)
```
